# Optimizing a Trainium2 kernel written in Bass

```python
import numpy as np
import jax
import jax.numpy as jnp

def _softmax(x, axis=-1):
    return jax.nn.softmax(x, axis=axis)

def _gelu(x):
    return jax.nn.gelu(x, approximate=True)

def _silu(x):
    return jax.nn.silu(x)

def _sigmoid(x):
    return jax.nn.sigmoid(x)

def _layernorm(x, axis=-1, eps=1e-05):
    m = jnp.mean(x, axis=axis, keepdims=True)
    v = jnp.var(x, axis=axis, keepdims=True)
    return (x - m) / jnp.sqrt(v + eps)

def _scatter_add(tgt, idx, src, axis=0):
    return tgt.at[idx].add(src)

def _segment_sum(src, seg, n):
    return jax.ops.segment_sum(src, seg, n)
kernel_name = 'mk_adaln_d1_jaxref_r8_98c7db'

def setup_inputs(seed: int=0):
    np.random.seed(seed)
    _w = jnp.asarray

    def _L0_attn_setup():
        import jax, jax.numpy as jnp
        import numpy as np
        DIM = 128
        HEADS = 16
        HEAD_DIM = DIM // HEADS
        COLLAPSE_THRESHOLD = 0.27
        SHARPNESS = 15.0
        LN_EPS = 1e-05
        NORM_EPS = 1e-12

        def _layernorm(x, gamma, beta):
            mu = jnp.mean(x, axis=-1, keepdims=True)
            var = jnp.mean(jnp.square(x - mu), axis=-1, keepdims=True)
            return (x - mu) * jax.lax.rsqrt(var + LN_EPS) * gamma + beta

        def _l2_normalize(x):
            n = jnp.sqrt(jnp.sum(jnp.square(x), axis=-1, keepdims=True))
            return x / jnp.maximum(n, NORM_EPS)
        key = jax.random.key(seed)
        ks = jax.random.split(key, 9)
        B, T = (2, 256)
        s = 1.0 / np.sqrt(DIM)
        sh = 1.0 / np.sqrt(HEAD_DIM)
        return {'x': jax.random.normal(ks[0], (B, T, DIM), dtype=jnp.float32), 'w_q': jax.random.normal(ks[1], (DIM, DIM), dtype=jnp.float32) * s, 'w_k': jax.random.normal(ks[2], (DIM, DIM), dtype=jnp.float32) * s, 'w_v': jax.random.normal(ks[3], (DIM, DIM), dtype=jnp.float32) * s, 'g_q': jax.random.normal(ks[4], (HEAD_DIM,), dtype=jnp.float32) * sh, 'g_k': jax.random.normal(ks[5], (HEAD_DIM,), dtype=jnp.float32) * sh, 'w_o': jax.random.normal(ks[6], (DIM, DIM), dtype=jnp.float32) * s, 'b_o': jnp.zeros((DIM,), dtype=jnp.float32), 'gamma': jnp.ones((DIM,), dtype=jnp.float32), 'beta': jnp.zeros((DIM,), dtype=jnp.float32)}
    _L0_attn_in = _L0_attn_setup()

    def _L0_ffn_setup():
        import jax, jax.numpy as jnp
        import numpy as np
        D, F, E, K = (128, 344, 8, 2)
        key = jax.random.key(seed)
        k0, k1, k2, k3, k4 = jax.random.split(key, 5)
        s = 0.02
        x = jax.random.normal(k0, (2, 64, D), jnp.float32)
        Ws = jax.random.normal(k1, (D, E), jnp.float32) * s
        bs = jnp.zeros((E,), jnp.float32)
        Wg = jax.random.normal(k2, (E, D, F), jnp.float32) * s
        Wu = jax.random.normal(k3, (E, D, F), jnp.float32) * s
        Wd = jax.random.normal(k4, (E, F, D), jnp.float32) * s
        return {'x': x, 'Ws': Ws, 'bs': bs, 'Wg': Wg, 'Wu': Wu, 'Wd': Wd}
    _L0_ffn_in = _L0_ffn_setup()
    _L0_c = _w((lambda *s: np.random.randn(*s).astype(np.float32) * 0.05)(4, 128))
    _L0_wmod = _w((lambda *s: np.random.randn(*s).astype(np.float32) * 0.05)(128, 6 * 128) * 128 ** (-0.5))
    _d = {'L0_attn_x': _L0_attn_in['x'], 'L0_attn_w_q': _L0_attn_in['w_q'], 'L0_attn_w_k': _L0_attn_in['w_k'], 'L0_attn_w_v': _L0_attn_in['w_v'], 'L0_attn_g_q': _L0_attn_in['g_q'], 'L0_attn_g_k': _L0_attn_in['g_k'], 'L0_attn_w_o': _L0_attn_in['w_o'], 'L0_attn_b_o': _L0_attn_in['b_o'], 'L0_attn_gamma': _L0_attn_in['gamma'], 'L0_attn_beta': _L0_attn_in['beta'], 'L0_ffn_Ws': _L0_ffn_in['Ws'], 'L0_ffn_bs': _L0_ffn_in['bs'], 'L0_ffn_Wg': _L0_ffn_in['Wg'], 'L0_ffn_Wu': _L0_ffn_in['Wu'], 'L0_ffn_Wd': _L0_ffn_in['Wd'], 'L0_c': _L0_c, 'L0_wmod': _L0_wmod}
    _x0 = _d['L0_attn_x']
    _d['L0_attn_x'] = jax.random.normal(jax.random.fold_in(jax.random.key(seed), 1), (4, 512, 128), dtype=_x0.dtype)
    del _x0
    return _d

def reference(L0_attn_x, L0_attn_w_q, L0_attn_w_k, L0_attn_w_v, L0_attn_g_q, L0_attn_g_k, L0_attn_w_o, L0_attn_b_o, L0_attn_gamma, L0_attn_beta, L0_ffn_Ws, L0_ffn_bs, L0_ffn_Wg, L0_ffn_Wu, L0_ffn_Wd, L0_c, L0_wmod):

    def _L0_attn_ref(x, w_q, w_k, w_v, g_q, g_k, w_o, b_o, gamma, beta):
        import jax, jax.numpy as jnp
        import numpy as np
        DIM = 128
        HEADS = 16
        HEAD_DIM = DIM // HEADS
        COLLAPSE_THRESHOLD = 0.27
        SHARPNESS = 15.0
        LN_EPS = 1e-05
        NORM_EPS = 1e-12

        def _layernorm(x, gamma, beta):
            mu = jnp.mean(x, axis=-1, keepdims=True)
            var = jnp.mean(jnp.square(x - mu), axis=-1, keepdims=True)
            return (x - mu) * jax.lax.rsqrt(var + LN_EPS) * gamma + beta

        def _l2_normalize(x):
            n = jnp.sqrt(jnp.sum(jnp.square(x), axis=-1, keepdims=True))
            return x / jnp.maximum(n, NORM_EPS)
        B, T, D = x.shape
        x_norm = _layernorm(x, gamma, beta)
        q = (x_norm @ w_q).reshape(B, T, HEADS, HEAD_DIM).transpose(0, 2, 1, 3)
        k = (x_norm @ w_k).reshape(B, T, HEADS, HEAD_DIM).transpose(0, 2, 1, 3)
        v = (x @ w_v).reshape(B, T, HEADS, HEAD_DIM).transpose(0, 2, 1, 3)
        q = _l2_normalize(q)
        k = _l2_normalize(k)
        align = jnp.einsum('bhqd,bhkd->bhqk', q, k)
        resonance = 0.5 + 0.5 * jnp.tanh((align - COLLAPSE_THRESHOLD) * SHARPNESS)
        gate_q = 0.25 + 0.75 * jax.nn.sigmoid(jnp.einsum('bhtd,d->bht', q, g_q))
        gate_k = 0.25 + 0.75 * jax.nn.sigmoid(jnp.einsum('bhtd,d->bht', k, g_k))
        modulation = resonance * gate_q[..., :, None] * gate_k[..., None, :]
        fused = jnp.einsum('bhqk,bhkd->bhqd', modulation, v)
        fused = fused.transpose(0, 2, 1, 3).reshape(B, T, HEADS * HEAD_DIM)
        return fused @ w_o + b_o

    def _L0_ffn_ref(x, Ws, bs, Wg, Wu, Wd):
        import jax, jax.numpy as jnp
        import numpy as np
        D, F, E, K = (128, 344, 8, 2)
        b, n, d = x.shape
        xt = x.reshape(-1, d)
        logits = xt @ Ws + bs
        topk_w, topk_idx = jax.lax.top_k(logits, K)
        topk_w = jax.nn.softmax(topk_w, axis=-1)
        combine = jnp.sum(jax.nn.one_hot(topk_idx, E, dtype=xt.dtype) * topk_w[..., None], axis=1)
        g = jnp.einsum('td,edf->tef', xt, Wg)
        u = jnp.einsum('td,edf->tef', xt, Wu)
        h = jax.nn.silu(g) * u
        y = jnp.einsum('tef,efd->ted', h, Wd)
        out = jnp.einsum('ted,te->td', y, combine)
        return out.reshape(b, n, d)
    x = L0_attn_x
    mod = (_silu(L0_c) @ L0_wmod).reshape(L0_c.shape[0], 6, 1, -1)
    sa, ca, ga, sb, cb, gb = (mod[:, 0], mod[:, 1], mod[:, 2], mod[:, 3], mod[:, 4], mod[:, 5])
    ga = (2 * (ga >= 0) - 1) * jnp.maximum(jnp.abs(ga), 0.25)
    gb = (2 * (gb >= 0) - 1) * jnp.maximum(jnp.abs(gb), 0.25)
    h = _layernorm(x, axis=-1) * (1 + ca) + sa
    x = x + ga * _L0_attn_ref(h, L0_attn_w_q, L0_attn_w_k, L0_attn_w_v, L0_attn_g_q, L0_attn_g_k, L0_attn_w_o, L0_attn_b_o, L0_attn_gamma, L0_attn_beta)
    h = _layernorm(x, axis=-1) * (1 + cb) + sb
    x = x + gb * _L0_ffn_ref(h, L0_ffn_Ws, L0_ffn_bs, L0_ffn_Wg, L0_ffn_Wu, L0_ffn_Wd)
    return x

_drawn_inputs = setup_inputs


def setup_inputs(seed=0):
    import zlib

    import numpy as np

    out = dict(_drawn_inputs(seed))
    spreads = {'L0_attn_b_o': (0.0, 0.587),
     'L0_attn_gamma': (1.0, 0.2),
     'L0_attn_beta': (0.0, 0.1),
     'L0_ffn_bs': (0.0, 0.8)}
    factors = {'L0_ffn_Ws': 8.0, 'L0_ffn_Wg': 8.0, 'L0_ffn_Wu': 8.0, 'L0_ffn_Wd': 8.0}
    for name, (base, spread) in spreads.items():
        noise = np.random.default_rng([zlib.crc32(name.encode()), seed]).standard_normal(out[name].shape)
        drawn = base * np.exp(spread * noise) if base else spread * noise
        out[name] = jnp.asarray(drawn.astype(out[name].dtype))
    for name, factor in factors.items():
        out[name] = (out[name] * factor).astype(out[name].dtype)
    return out
```

```python
from contextlib import ExitStack

import concourse.bass as bass
from concourse import mybir

ALU = mybir.AluOpType
ACT = mybir.ActivationFunctionType
AX_X = mybir.AxisListType.X
F32 = mybir.dt.float32
F32R = mybir.dt.float32r
I32 = mybir.dt.int32
U32 = mybir.dt.uint32

P = 128
HEADS = 16
QUADS = 4
LANES = 4
THRESHOLD = 0.27
SHARPNESS = 15.0
LN_EPS = 1e-5
NORM_EPS = 1e-12
RSQRT_MAGIC = 0x5F3759DF


def adaln_block(nc, x, w_q, w_k, w_v, g_q, g_k, w_o, b_o, gamma, beta, Ws, bs, Wg, Wu, Wd, c, wmod, out):
    B, T, D = x.shape
    HD = D // HEADS
    TT = T // P
    E, _, F = Wg.shape
    FC = -(-F // P)
    FLAST = F - (FC - 1) * P
    NT = B * TT
    STEPS = QUADS * TT
    assert D == P and HD == 8 and T == TT * P and LANES * QUADS == HEADS and TT == 4

    ctx = ExitStack()
    with ctx:
        def sb(name, shape, dt=F32):
            return ctx.enter_context(nc.sbuf_tensor(name, shape, dt))

        def sem(name):
            return ctx.enter_context(nc.semaphore(name))

        tanh = sb("tanh", [P, 4, 2, T])
        wm = tanh[:, 0].rearrange("p a t -> p (a t)")[:, 0:6 * D]
        silub = tanh[:, 1].rearrange("p a t -> p (a t)")[:, 0:B * P].rearrange("p (b q) -> p b q", b=B)
        sg = tanh[:, 2, :, 0:F]
        hid = tanh[:, 3, :, 0:FC * P]
        ident = sb("ident", [P, P])
        ones = sb("ones", [P, 1])
        mhalf = sb("mhalf", [P, TT])
        tanh_bias = sb("tanh_bias", [P, 1])
        wqk = sb("wqk", [P, 2, D])
        wv = sb("wv", [P, D])
        wvp = sb("wvp", [P, D])
        wo = sb("wo", [P, D])
        ws = sb("ws", [P, E])
        bsb = sb("bsb", [P, E])
        gqk = sb("gqk", [P, 2, HD])
        gam = sb("gam", [P, 1])
        bet = sb("bet", [P, 1])
        bo = sb("bo", [P, D])
        cT = sb("cT", [P, B])
        siluc = sb("siluc", [P, B])
        mod = sb("mod", [P, B, 6, D])
        mtmp = sb("mtmp", [P, 2, D])
        gab = sb("gab", [P, B, D])
        wgh = sb("wgh", [P, E, F], F32R)
        wgl = sb("wgl", [P, E, F], F32R)
        wuh = sb("wuh", [P, E, F], F32R)
        wul = sb("wul", [P, E, F], F32R)
        wdh = sb("wdh", [P, E, FC, D], F32R)
        wdl = sb("wdl", [P, E, FC, D], F32R)
        wraw = sb("wraw", [P, 2, FC * D])
        iota8 = sb("iota8", [P, E])
        xin = sb("xin", [P, B, TT, D])
        x1 = xin
        h2T = sb("h2T", [P, TT, D])
        h2h = sb("h2h", [P, NT, P], F32R)
        h2l = sb("h2l", [P, NT, P], F32R)
        lg = sb("lg", [P, NT, E])
        st = sb("st", [P, TT, 6])
        mv = sb("mv", [P, TT, 2])
        ve = sb("ve", [P, TT])
        rstd = sb("rstd", [P, TT])
        hh = sb("hh", [P, TT, D])
        hn = sb("hn", [P, TT, D])
        hT = sb("hT", [P, TT, P])
        xnT = sb("xnT", [P, TT, P])
        qkv = sb("qkv", [P, 3, TT, D])
        sq = sb("sq", [P, 2, TT, D])
        ss = sb("ss", [P, 2 * TT * HEADS])
        yr = sb("yr", [P, 2 * TT * HEADS])
        yt = sb("yt", [P, 2 * TT * HEADS])
        qn = qkv[:, 0:2]
        ex = sb("ex", [P, 2, TT, HEADS, 2, 2, HD])
        dots = sb("dots", [P, 2, TT, HEADS])
        gt = sb("gt", [P, 2, TT, HEADS])
        gate = sb("gate", [P, 2, TT, HEADS])
        gqe = sb("gqe", [P, TT, D])
        gv = sb("gv", [P, TT, D])
        gvz = sb("gvz", [P, TT, QUADS, LANES, 32])
        QA = sb("QA", [P, QUADS, TT * P], F32R)
        KA = sb("KA", [P, QUADS, TT * P], F32R)
        GQT = sb("GQT", [P, TT * P])
        Cs = sb("Cs", [P, 1])
        fT = sb("fT", [P, TT * P])
        xb = sb("xb", [P, TT, D])
        st2 = sb("st2", [P, TT, 6])
        mv2 = sb("mv2", [P, TT, 2])
        ve2 = sb("ve2", [P, TT])
        rstd2 = sb("rstd2", [P, TT])
        h2 = sb("h2", [P, TT, D])
        topi = sb("topi", [P, NT, 8], U32)
        free = sq[:].rearrange("p a t d -> p (a t d)")
        top = free[:, 0:NT * 8].rearrange("p (t k) -> p t k", k=8)
        topf = free[:, NT * 8:NT * 16].rearrange("p (t k) -> p t k", k=8)
        wts = free[:, NT * 16:NT * 24].rearrange("p (t k) -> p t k", k=8)
        oh = free[:, NT * 24:NT * 40].rearrange("p (a t k) -> p a t k", a=2, k=8)
        w12 = free[:, NT * 40:NT * 42].rearrange("p (a t) -> p a t", a=2)
        dl = free[:, NT * 42:NT * 43]
        th = free[:, NT * 43:NT * 44]
        ytmp = sb("ytmp", [P, D])
        hTh = QA[:, 0:2, 0:FC * P].rearrange("p a (k q) -> p a k q", k=FC)
        hTl = KA[:, 0:2, 0:FC * P].rearrange("p a (k q) -> p a k q", k=FC)

        S = ctx.enter_context(nc.psum_tensor("S", [P, 2, 2, 512], F32))
        AV = ctx.enter_context(nc.psum_tensor("AV", [P, 512], F32))
        R = ctx.enter_context(nc.psum_tensor("R", [P, 3, 512], F32))

        s_c, s_wm, s_wqkv, s_small, s_bo = sem("s_c"), sem("s_wm"), sem("s_wqkv"), sem("s_small"), sem("s_bo")
        s_x = [sem(f"s_x{b}") for b in range(B)]
        s_wo = sem("s_wo")
        s_raw = [sem("s_raw0"), sem("s_raw1")]
        out_stored = sem("out_stored")
        ident_ready = sem("ident_ready")
        consts_ready = sem("consts_ready")
        silu_c_ready = sem("silu_c_ready")
        silu_b_ready = sem("silu_b_ready")
        mod_ps = sem("mod_ps")
        mod_ready = sem("mod_ready")
        wvp_ready = sem("wvp_ready")
        gab_ready = sem("gab_ready")
        dve_chain = sem("dve_chain")
        pool_chain = sem("pool_chain")
        var_ready = sem("var_ready")
        rstd_ready = sem("rstd_ready")
        hn_ready = sem("hn_ready")
        xT_ready = sem("xT_ready")
        qkv_ready = sem("qkv_ready")
        sq_ready = sem("sq_ready")
        rn_ready = sem("rn_ready")
        qn_ready = sem("qn_ready")
        prod_ready = sem("prod_ready")
        hi_ready = sem("hi_ready")
        lo_ready = sem("lo_ready")
        dots_ready = sem("dots_ready")
        gt_ready = sem("gt_ready")
        gate_ready = sem("gate_ready")
        gv_ready = sem("gv_ready")
        gqe_ready = sem("gqe_ready")
        gvz_ready = sem("gvz_ready")
        ring_full = sem("ring_full")
        ring_free = sem("ring_free")
        operand_ready = sem("operand_ready")
        scores_ready = sem("scores_ready")
        tanh_ready = sem("tanh_ready")
        av_done = sem("av_done")
        fused_ready = sem("fused_ready")
        xb_ready = sem("xb_ready")
        var2_ready = sem("var2_ready")
        rstd2_ready = sem("rstd2_ready")
        xh2_ready = sem("xh2_ready")
        h2_ready = sem("h2_ready")
        h2l_ready = sem("h2l_ready")
        split_ready = sem("split_ready")
        wsplit = sem("wsplit")
        wlo = sem("wlo")
        dl_ready = sem("dl_ready")
        th_ready = sem("th_ready")
        gu_ready = sem("gu_ready")
        silu_ready = sem("silu_ready")
        hid_ready = sem("hid_ready")
        hidT_ps = sem("hidT_ps")
        hTh_ready = sem("hTh_ready")
        hTl_ready = sem("hTl_ready")
        down_done = sem("down_done")
        y_ready = sem("y_ready")
        yo_ready = sem("yo_ready")

        xs = x.rearrange("b (p t) d -> p b t d", t=TT)
        outs = out.rearrange("b (p t) d -> p b t d", t=TT)
        NW = 2 * E

        def copies(a, u):
            e4 = ex[:, a].rearrange("p t h u v d -> p (t h) u v d")
            return (e4[:, :, 0, u], e4[:, :, 1, u]) if a == 0 else (e4[:, :, u, 0], e4[:, :, u, 1])

        block = ctx.enter_context(nc.Block())

        USE = {}
        order = []

        def use(*key):
            USE[key] = len(order)
            order.append(key)

        def start_uses(b):
            use("h", b)
            use("hn", b)

        def qkv_uses(b):
            for tt in range(TT):
                use("qkv", b, tt)

        def gate_uses(b):
            use("gate", b)
            use("csum", b)

        def operand_uses(b):
            for i in range(QUADS):
                use("q", b, i)
                use("k", b, i)

        def post_uses(b):
            use("wo", b)
            use("h2T", b)
            use("logit", b)

        for b in range(B):
            use("mod", b, 0)
            use("mod", b, 1)
        start_uses(0)
        qkv_uses(0)
        operand_uses(0)
        for b in range(B):
            if b + 1 < B:
                start_uses(b + 1)
            gate_uses(b)
            if b + 1 < B:
                qkv_uses(b + 1)
            if b >= 1:
                post_uses(b - 1)
            if b + 1 < B:
                operand_uses(b + 1)
        post_uses(B - 1)

        @block.sync
        def _(sp):
            sp.dma_start(wm[:], wmod).then_inc(s_wm, 16)
            sp.dma_start(xin[:, 0], xs[:, 0]).then_inc(s_x[0], 16)
            sp.dma_start(wqk[:, 0], w_q).then_inc(s_wqkv, 16)
            sp.dma_start(wqk[:, 1], w_k).then_inc(s_wqkv, 16)
            sp.dma_start(wv[:], w_v).then_inc(s_wqkv, 16)
            for lane in range(LANES):
                src = w_o.rearrange("(i j d) n -> j i d n", i=QUADS, j=LANES)[lane]
                for i in range(QUADS):
                    r0 = 32 * lane + HD * i
                    sp.dma_start(wo[r0:r0 + HD, :], src[i]).then_inc(s_wo, 16)
            for b in range(1, B):
                sp.dma_start(xin[:, b], xs[:, b]).then_inc(s_x[b], 16)
            sp.dma_start(bo[:], b_o.partition_broadcast(P)).then_inc(s_bo, 16)
            sp.wait_ge(consts_ready, 1)
            for n in range(3 * E):
                if n >= 2:
                    sp.wait_ge(wlo, n - 1)
                if n < NW:
                    W = Wg if n < E else Wu
                    sp.dma_start(wraw[:, n % 2, 0:F], W[n % E]).then_inc(s_raw[n % 2], 16)
                else:
                    e = n - NW
                    sp.dma_start(wraw[:, n % 2, 0:(FC - 1) * D],
                                 Wd[e, 0:(FC - 1) * P].rearrange("(k p) d -> p k d", p=P)).then_inc(s_raw[n % 2], 16)
                    sp.dma_start(wraw[0:FLAST, n % 2, (FC - 1) * D:FC * D],
                                 Wd[e, (FC - 1) * P:F]).then_inc(s_raw[n % 2], 16)
            for t in range(NT):
                sp.wait_ge(yo_ready, t + 1)
                sp.dma_start(outs[:, t // TT, t % TT], x1[:, t // TT, t % TT]).then_inc(out_stored, 16)
            sp.wait_ge(out_stored, 16 * NT)

        @block.gpsimd
        def _(pool):
            g = nc.gpsimd
            chain = [0]

            def link(ins):
                chain[0] += 1
                ins.then_inc(pool_chain, 1)
                pool.wait_ge(pool_chain, chain[0])

            link(g.memset(ident[:], 0.0))
            g.affine_select(out=ident[:], in_=ident[:], compare_op=ALU.not_equal, fill=1.0, base=0,
                            pattern=[[-1, P]], channel_multiplier=1).then_inc(ident_ready, 1)
            g.memset(mhalf[:], -0.5)
            g.memset(gvz[:], 0.0)
            g.memset(wraw[:], 0.0)
            g.memset(tanh_bias[:], -THRESHOLD * SHARPNESS)
            g.memset(ones[:], 1.0)
            g.iota(iota8[:], [[1, E]], base=0, channel_multiplier=0,
                   allow_small_or_imprecise_dtypes=True).then_inc(consts_ready, 1)
            pool.wait_ge(s_wqkv, 48)
            g.tensor_copy(wvp[:].rearrange("p (j i d) -> p i j d", j=LANES, i=QUADS),
                          wv[:].rearrange("p (i j d) -> p i j d", i=QUADS, j=LANES)).then_inc(wvp_ready, 1)

            def power(dst, src, ready, n):
                pool.wait_ge(ready, n)
                return g.tensor_tensor(dst, src, mhalf[:], ALU.pow)

            def weights(n):
                pool.wait_ge(wsplit, n + 1)
                if n < NW:
                    hi, lo = ((wgh, wgl), (wuh, wul))[n // E]
                    e = n % E
                    g.tensor_tensor(lo[:, e], wraw[:, n % 2, 0:F], hi[:, e].bitcast(F32),
                                    ALU.subtract).then_inc(wlo, 1)
                else:
                    e = n - NW
                    g.tensor_tensor(wdl[:, e].rearrange("p k d -> p (k d)"), wraw[:, n % 2],
                                    wdh[:, e].rearrange("p k d -> p (k d)").bitcast(F32),
                                    ALU.subtract).then_inc(wlo, 1)

            def norms(b):
                power(rstd[:], ve[:], var_ready, 2 * b + 1).then_inc(rstd_ready, 1)
                power(rstd[:], ve[:], var_ready, 2 * b + 2).then_inc(rstd_ready, 1)

            def squares(b):
                pool.wait_ge(ring_free, USE[("qkv", b, TT - 1)] + 1)
                if b >= 1:
                    pool.wait_ge(dots_ready, b)
                g.tensor_tensor(sq[:], qkv[:, 0:2], qkv[:, 0:2], ALU.mult).then_inc(sq_ready, 1)

            def unit_qk(b):
                pool.wait_ge(rn_ready, b + 1)
                g.tensor_tensor(qn[:].rearrange("p a t (h d) -> p (a t h) d", d=HD),
                                qkv[:, 0:2].rearrange("p a t (h d) -> p (a t h) d", d=HD),
                                yr[:].unsqueeze(2).to_broadcast([P, 2 * TT * HEADS, HD]),
                                ALU.mult).then_inc(qn_ready, 1)
                pool.wait_ge(qn_ready, b + 1)
                for a in range(2):
                    last = g.tensor_tensor(sq[:, a].rearrange("p t (h d) -> p (t h) d", d=HD),
                                           qn[:, a].rearrange("p t (h d) -> p (t h) d", d=HD),
                                           gqk[:, a].unsqueeze(1).to_broadcast([P, TT * HEADS, HD]), ALU.mult)
                last.then_inc(prod_ready, 1)

            def lo_parts(b):
                pool.wait_ge(hi_ready, b + 1)
                for a in range(2):
                    src = qn[:, a].rearrange("p t (h d) -> p (t h) d", d=HD)
                    for u in range(2):
                        hi, dst = copies(a, u)
                        last = g.tensor_tensor(dst, src, hi, ALU.subtract)
                last.then_inc(lo_ready, 1)

            def gated(b):
                pool.wait_ge(gate_ready, b + 1)
                if b >= 1:
                    pool.wait_ge(ring_full, USE[("csum", b - 1)] + 1)
                for tt in range(TT):
                    gk = gate[:, 1, tt].rearrange("p (i j) -> p j i", j=LANES)
                    last = g.tensor_tensor(gv[:, tt].rearrange("p (j i d) -> p j i d", j=LANES, d=HD),
                                           qkv[:, 2, tt].rearrange("p (j i d) -> p j i d", j=LANES, d=HD),
                                           gk.unsqueeze(3).to_broadcast([P, LANES, QUADS, HD]), ALU.mult)
                last.then_inc(gv_ready, 1)
                for tt in range(TT):
                    gq = gate[:, 0, tt].rearrange("p (i j) -> p j i", j=LANES)
                    last = g.tensor_copy(gqe[:, tt].rearrange("p (j i d) -> p j i d", j=LANES, d=HD),
                                         gq.unsqueeze(3).to_broadcast([P, LANES, QUADS, HD]))
                last.then_inc(gqe_ready, 1)

            def value_operand(b, i):
                pool.wait_ge(gv_ready, b + 1)
                if b >= 1:
                    pool.wait_ge(av_done, STEPS * (b - 1) + TT * (i + 1))
                g.tensor_copy(gvz[:, :, i, :, HD * i:HD * (i + 1)],
                              gv[:].rearrange("p t (j i d) -> p t j i d", j=LANES, d=HD)[:, :, :, i]
                              ).then_inc(gvz_ready, 1)

            def residual(b):
                if b >= 1:
                    pool.wait_ge(var2_ready, b)
                g.tensor_tensor(xb[:], xin[:, b], gab[:, b].unsqueeze(1).to_broadcast([P, TT, D]),
                                ALU.add).then_inc(xb_ready, 1)

            def modulate(b):
                pool.wait_ge(xh2_ready, b + 1)
                link(g.tensor_tensor(h2[:], h2[:], mod[:, b, 4].unsqueeze(1).to_broadcast([P, TT, D]), ALU.mult))
                g.tensor_tensor(h2[:], h2[:], mod[:, b, 3].unsqueeze(1).to_broadcast([P, TT, D]),
                                ALU.add).then_inc(h2_ready, 1)

            def h2_lo(b):
                pool.wait_ge(split_ready, b + 1)
                g.tensor_tensor(h2l[:, TT * b:TT * (b + 1)], h2T[:],
                                h2h[:, TT * b:TT * (b + 1)].bitcast(F32), ALU.subtract).then_inc(h2l_ready, 1)

            def norm2(b):
                power(rstd2[:], ve2[:], var2_ready, b + 1).then_inc(rstd2_ready, 1)

            pool.wait_ge(mod_ready, 1)
            pool.wait_ge(s_bo, 16)
            for b in range(B):
                g.tensor_tensor(gab[:, b], mod[:, b, 2], bo[:], ALU.mult).then_inc(gab_ready, 1)
            pool.wait_ge(s_small, 16 * 6)
            pool.wait_ge(gab_ready, B)
            norms(0)
            squares(0)
            unit_qk(0)
            lo_parts(0)
            gated(0)
            for i in range(QUADS):
                value_operand(0, i)
            norms(1)
            n = 0
            for b in range(B):
                more = b + 1 < B
                if b >= 1:
                    residual(b - 1)
                if more:
                    squares(b + 1)
                if b >= 1:
                    norm2(b - 1)
                if more:
                    unit_qk(b + 1)
                if b >= 1:
                    modulate(b - 1)
                if more:
                    lo_parts(b + 1)
                for _ in range(3 * E // B):
                    weights(n)
                    n += 1
                if b >= 1:
                    h2_lo(b - 1)
                if more:
                    gated(b + 1)
                    for i in range(QUADS - 1):
                        value_operand(b + 1, i)
                if b + 2 < B:
                    norms(b + 2)
                if more:
                    value_operand(b + 1, QUADS - 1)
            residual(B - 1)
            norm2(B - 1)
            modulate(B - 1)
            h2_lo(B - 1)

        @block.scalar
        def _(act):
            a = nc.scalar
            with nc.allow_non_contiguous_dma(reason="small transposed and column loads"):
                act.dma_start(cT[:], c.rearrange("b d -> d b")).then_inc(s_c, 16)
                act.dma_start(gam[:], gamma.rearrange("(d a) -> d a", a=1)).then_inc(s_small, 16)
                act.dma_start(bet[:], beta.rearrange("(d a) -> d a", a=1)).then_inc(s_small, 16)
            act.dma_start(gqk[:, 0], g_q.partition_broadcast(P)).then_inc(s_small, 16)
            act.dma_start(gqk[:, 1], g_k.partition_broadcast(P)).then_inc(s_small, 16)
            act.dma_start(ws[:], Ws).then_inc(s_small, 16)
            act.dma_start(bsb[:], bs.partition_broadcast(P)).then_inc(s_small, 16)
            act.wait_ge(s_c, 16)
            a.activation(siluc[:], cT[:], ACT.Silu).then_inc(silu_c_ready, 1)

            def gates(b):
                act.wait_ge(dots_ready, b + 1)
                if b >= 1:
                    act.wait_ge(gate_ready, b)
                a.activation(gt[:], dots[:], ACT.Tanh, scale=0.5).then_inc(gt_ready, 1)

            gates(0)
            act.wait_ge(consts_ready, 1)
            for b in range(B):
                for s in range(STEPS):
                    for pr in range(2):
                        n = 2 * (STEPS * b + s) + pr
                        act.wait_ge(scores_ready, n + 1)
                        if n >= 4:
                            act.wait_ge(av_done, (n - 4) // 2 + 1)
                        a.activation(tanh[:, n % 4], S[:, pr], ACT.Tanh, bias=tanh_bias[:, 0:1],
                                     scale=SHARPNESS).then_inc(tanh_ready, 1)
                    if s == 11 and b + 1 < B:
                        gates(b + 1)
            act.wait_ge(dl_ready, 1)
            a.activation(th, dl, ACT.Tanh, scale=0.5).then_inc(th_ready, 1)
            for n in range(NT * E):
                act.wait_ge(gu_ready, n + 1)
                if n >= 2:
                    act.wait_ge(hid_ready, n - 1)
                a.activation(sg[:, n % 2], S[:, n % 2, 0, 0:F], ACT.Silu).then_inc(silu_ready, 1)

        @block.vector
        def _(dve):
            v = nc.vector
            chain = [0]

            def link(ins):
                chain[0] += 1
                ins.then_inc(dve_chain, 1)
                dve.wait_ge(dve_chain, chain[0])

            def full(*key):
                dve.wait_ge(ring_full, USE[key] + 1)
                return R[:, USE[key] % 3]

            dve.wait_ge(silu_c_ready, 1)
            v.tensor_copy(silub, siluc[:].unsqueeze(2).to_broadcast([P, B, P])).then_inc(silu_b_ready, 1)
            for b in range(B):
                for half in range(2):
                    r = full("mod", b, half)
                    v.tensor_copy(mod[:, b, 3 * half:3 * half + 3].rearrange("p a d -> p (a d)"),
                                  r[:, 0:3 * D]).then_inc(ring_free, 1)
            dve.wait_ge(ring_free, 2 * B)
            for b in range(B):
                for half in range(2):
                    m = mod[:, b, 3 * half:3 * half + 3]
                    v.tensor_scalar(m[:, 1], m[:, 1], 1.0, None, ALU.add)
                    v.tensor_scalar(mtmp[:, 0], m[:, 2], 0.0, 0.5, ALU.is_ge, ALU.subtract)
                    link(v.scalar_tensor_tensor(mtmp[:, 1], m[:, 2], -1.0, m[:, 2], ALU.mult, ALU.max))
                    link(v.tensor_scalar(mtmp[:, 1], mtmp[:, 1], 0.25, 2.0, ALU.max, ALU.mult))
                    last = v.tensor_tensor(m[:, 2], mtmp[:, 0], mtmp[:, 1], ALU.mult)
                    if b == B - 1 and half == 1:
                        last.then_inc(mod_ready, 1)
                    else:
                        link(last)

            def stats(src, st, mv, ve, var_sem):
                for tt in range(TT):
                    last = v.bn_stats(st[:, tt], src[:, tt])
                link(last)
                for tt in range(TT):
                    last = v.bn_aggr(mv[:, tt], st[:, tt])
                link(last)
                v.tensor_scalar(ve[:], mv[:, :, 1], LN_EPS, None, ALU.add).then_inc(var_sem, 1)

            def normalize(dst, src, mv, rstd, ready, n):
                dve.wait_ge(ready, n)
                for tt in range(TT):
                    last = v.tensor_scalar(dst[:, tt], src[:, tt], mv[:, tt, 0:1], rstd[:, tt:tt + 1],
                                           ALU.subtract, ALU.mult)
                return last

            def prep_norms(b):
                dve.wait_ge(s_x[b], 16)
                dve.wait_ge(mod_ready, 1)
                stats(xin[:, b], st, mv, ve, var_ready)
                if b >= 1:
                    dve.wait_ge(ring_full, USE[("hn", b - 1)] + 1)
                link(normalize(hh, xin[:, b], mv, rstd, rstd_ready, 2 * b + 1))
                link(v.tensor_tensor(hh[:], hh[:], mod[:, b, 1].unsqueeze(1).to_broadcast([P, TT, D]), ALU.mult))
                link(v.tensor_tensor(hh[:], hh[:], mod[:, b, 0].unsqueeze(1).to_broadcast([P, TT, D]), ALU.add))
                stats(hh, st, mv, ve, var_ready)
                normalize(hn, hh, mv, rstd, rstd_ready, 2 * b + 2).then_inc(hn_ready, 1)

            def prep_xT(b):
                dve.wait_ge(s_small, 96)
                r = full("h", b)
                if b >= 1:
                    dve.wait_ge(ring_full, USE[("qkv", b - 1, TT - 1)] + 1)
                v.tensor_copy(hT[:].rearrange("p t d -> p (t d)"), r[:]).then_inc(ring_free, 1)
                r = full("hn", b)
                v.tensor_scalar(xnT[:].rearrange("p t d -> p (t d)"), r[:], gam[:, 0:1], bet[:, 0:1], ALU.mult,
                                ALU.add).then_inc(ring_free, 1)

            def prep_qkv(b):
                if b >= 1:
                    dve.wait_ge(gv_ready, b)
                for tt in range(TT):
                    r = full("qkv", b, tt)
                    v.tensor_copy(qkv[:, :, tt], r[:, 0:3 * D].rearrange("p (a d) -> p a d", a=3)
                                  ).then_inc(ring_free, 1)

            def prep_rn(b):
                dve.wait_ge(sq_ready, b + 1)
                link(v.tensor_reduce(ss[:], sq[:].rearrange("p a t (h d) -> p (a t h) d", d=HD), AX_X, ALU.add))
                link(v.tensor_scalar(ss[:], ss[:], NORM_EPS * NORM_EPS, None, ALU.max))
                link(v.tensor_scalar(yt[:].bitcast(I32), ss[:].bitcast(I32), 1, None, ALU.arith_shift_right))
                if b >= 1:
                    dve.wait_ge(qn_ready, b)
                link(v.tensor_scalar(yr[:].bitcast(I32), yt[:].bitcast(I32), -1.0, float(RSQRT_MAGIC),
                                     ALU.mult, ALU.add))
                for it in range(3):
                    link(v.tensor_tensor(yt[:], yr[:], yr[:], ALU.mult))
                    link(v.tensor_tensor(yt[:], yt[:], ss[:], ALU.mult))
                    link(v.tensor_scalar(yt[:], yt[:], -0.5, 1.5, ALU.mult, ALU.add))
                    last = v.tensor_tensor(yr[:], yr[:], yt[:], ALU.mult)
                    if it < 2:
                        link(last)
                last.then_inc(rn_ready, 1)

            def prep_hi(b):
                dve.wait_ge(qn_ready, b + 1)
                if b >= 1:
                    dve.wait_ge(ring_full, USE[("k", b - 1, QUADS - 1)] + 1)
                for a in range(2):
                    src = qn[:, a].rearrange("p t (h d) -> p (t h) d", d=HD)
                    for u in range(2):
                        last = v.tensor_copy(copies(a, u)[0].bitcast(F32R), src)
                last.then_inc(hi_ready, 1)
                dve.wait_ge(prod_ready, b + 1)
                v.tensor_reduce(dots[:].rearrange("p a t h -> p (a t h)"),
                                sq[:].rearrange("p a t (h d) -> p (a t h) d", d=HD), AX_X, ALU.add
                                ).then_inc(dots_ready, 1)

            def prep_gates(b):
                dve.wait_ge(gt_ready, b + 1)
                if b >= 1:
                    dve.wait_ge(gqe_ready, b)
                v.tensor_scalar(gate[:, 0], gt[:, 0], 0.375, 0.625, ALU.mult, ALU.add)
                v.tensor_scalar(gate[:, 1], gt[:, 1], 0.1875, 0.3125, ALU.mult, ALU.add).then_inc(gate_ready, 1)

            def prep_gqt(b):
                r = full("gate", b)
                v.tensor_copy(GQT[:], r[:]).then_inc(ring_free, 1)
                r = full("csum", b)
                v.tensor_copy(Cs[:], r[:, 0:1]).then_inc(ring_free, 1)

            def prep_operands(b, i):
                if b >= 1:
                    dve.wait_ge(scores_ready, 2 * (STEPS * (b - 1) + TT * (i + 1)))
                r = full("q", b, i)
                v.tensor_copy(QA[:, i], r[:]).then_inc(ring_free, 1)
                r = full("k", b, i)
                v.tensor_copy(KA[:, i], r[:]).then_inc(ring_free, 1)

            def fuse(b):
                dve.wait_ge(av_done, STEPS * (b + 1))
                if b >= 1:
                    dve.wait_ge(ring_full, USE[("wo", b - 1)] + 1)
                dve.wait_ge(ring_free, USE[("csum", b)] + 1)
                v.scalar_tensor_tensor(fT[:], AV[:], Cs[:, 0:1], GQT[:], ALU.add, ALU.mult).then_inc(fused_ready, 1)

            def post_x1(b):
                r = full("wo", b)
                dve.wait_ge(xb_ready, b + 1)
                v.tensor_tensor(x1[:, b], r[:].rearrange("p (t d) -> p t d", t=TT),
                                mod[:, b, 2].unsqueeze(1).to_broadcast([P, TT, D]), ALU.mult).then_inc(ring_free, 1)
                dve.wait_ge(ring_free, USE[("wo", b)] + 1)
                link(v.tensor_tensor(x1[:, b], x1[:, b], xb[:], ALU.add))
                stats(x1[:, b], st2, mv2, ve2, var2_ready)

            def post_norm(b):
                if b >= 1:
                    dve.wait_ge(ring_full, USE[("h2T", b - 1)] + 1)
                normalize(h2, x1[:, b], mv2, rstd2, rstd2_ready, b + 1).then_inc(xh2_ready, 1)

            def post_h2(b):
                r = full("h2T", b)
                if b >= 1:
                    dve.wait_ge(h2l_ready, b)
                v.tensor_copy(h2T[:].rearrange("p t d -> p (t d)"), r[:]).then_inc(ring_free, 1)
                dve.wait_ge(ring_free, USE[("h2T", b)] + 1)
                v.tensor_copy(h2h[:, TT * b:TT * (b + 1)], h2T[:]).then_inc(split_ready, 1)
                r = full("logit", b)
                v.tensor_tensor(lg[:, TT * b:TT * (b + 1)], r[:, 0:TT * E].rearrange("p (t e) -> p t e", e=E),
                                bsb[:].unsqueeze(1).to_broadcast([P, TT, E]), ALU.add).then_inc(ring_free, 1)

            def weights(n):
                dve.wait_ge(s_raw[n % 2], raw_count(n))
                if n < NW:
                    hi = (wgh, wuh)[n // E]
                    v.tensor_copy(hi[:, n % E], wraw[:, n % 2, 0:F]).then_inc(wsplit, 1)
                else:
                    v.tensor_copy(wdh[:, n - NW].rearrange("p k d -> p (k d)"), wraw[:, n % 2]).then_inc(wsplit, 1)

            def raw_count(n):
                return 16 * sum(1 if m < NW else 2 for m in range(n % 2, n + 1, 2))

            n = 0
            prep_norms(0)
            prep_xT(0)
            prep_qkv(0)
            prep_rn(0)
            prep_hi(0)
            prep_gates(0)
            for i in range(QUADS):
                prep_operands(0, i)
            prep_norms(1)
            dve.wait_ge(consts_ready, 1)
            for b in range(B):
                more = b + 1 < B
                if b >= 1:
                    fuse(b - 1)
                if more:
                    prep_xT(b + 1)
                prep_gqt(b)
                if more:
                    prep_qkv(b + 1)
                if b >= 1:
                    post_x1(b - 1)
                if more:
                    prep_rn(b + 1)
                if b >= 1:
                    post_norm(b - 1)
                if more:
                    prep_hi(b + 1)
                if b >= 1:
                    post_h2(b - 1)
                for _ in range(3 * E // B):
                    weights(n)
                    n += 1
                if more:
                    prep_gates(b + 1)
                    for i in range(QUADS - 1):
                        prep_operands(b + 1, i)
                if b + 2 < B:
                    prep_norms(b + 2)
                if more:
                    prep_operands(b + 1, QUADS - 1)
            fuse(B - 1)
            post_x1(B - 1)
            post_norm(B - 1)
            post_h2(B - 1)
            dve.wait_ge(ring_free, len(order))
            for t in range(NT):
                last = v.max(top[:, t], lg[:, t])
            link(last)
            for t in range(NT):
                last = v.max_index(topi[:, t], top[:, t], lg[:, t])
            link(last)
            v.tensor_tensor(dl, top[:, :, 0], top[:, :, 1], ALU.subtract).then_inc(dl_ready, 1)
            link(v.tensor_copy(topf, topi[:]))
            dve.wait_ge(th_ready, 1)
            v.tensor_scalar(w12[:, 0], th, 0.5, 0.5, ALU.mult, ALU.add)
            link(v.tensor_scalar(w12[:, 1], th, -0.5, 0.5, ALU.mult, ALU.add))
            for k in range(2):
                link(v.tensor_tensor(oh[:, k], iota8[:].unsqueeze(1).to_broadcast([P, NT, E]),
                                     topf[:, :, k:k + 1].to_broadcast([P, NT, E]), ALU.is_equal))
                link(v.tensor_tensor(oh[:, k], oh[:, k], w12[:, k].unsqueeze(2).to_broadcast([P, NT, E]), ALU.mult))
            link(v.tensor_tensor(wts, oh[:, 0], oh[:, 1], ALU.add))

            def finish(t):
                dve.wait_ge(down_done, E * (t + 1))
                y = R[:, t % 2, 0:D]
                x1t = x1[:, t // TT, t % TT]
                link(v.tensor_tensor(ytmp[:], y, mod[:, t // TT, 5], ALU.mult))
                v.tensor_tensor(x1t, ytmp[:], x1t, ALU.add).then_inc(yo_ready, 1)

            link(v.memset(hid[:, :, F:FC * P], 0.0))
            N = NT * E
            for n in range(N + 1):
                if n < N:
                    t, e = n // E, n % E
                    dve.wait_ge(silu_ready, n + 1)
                    if n >= 2:
                        dve.wait_ge(hidT_ps, n - 1)
                    v.scalar_tensor_tensor(hid[:, n % 2, 0:F], sg[:, n % 2], wts[:, t, e:e + 1], S[:, n % 2, 1, 0:F],
                                           ALU.mult, ALU.mult).then_inc(hid_ready, 1)
                if n >= 1:
                    m = n - 1
                    dve.wait_ge(hidT_ps, m + 1)
                    if m >= 2:
                        dve.wait_ge(down_done, m - 1)
                    ps = (AV, R[:, 2])[m % 2]
                    v.tensor_copy(hTh[:, m % 2].rearrange("p k d -> p (k d)"), ps[:, 0:FC * P]).then_inc(hTh_ready, 1)
                    dve.wait_ge(hTh_ready, m + 1)
                    v.tensor_tensor(hTl[:, m % 2].rearrange("p k d -> p (k d)"), ps[:, 0:FC * P],
                                    hTh[:, m % 2].rearrange("p k d -> p (k d)").bitcast(F32),
                                    ALU.subtract).then_inc(hTl_ready, 1)
                    if m % E == 2 and m >= E:
                        finish(m // E - 1)
            finish(NT - 1)

        @block.tensor
        def _(pe):
            mm = nc.tensor.matmul

            def claim(*key):
                n = USE[key]
                if n >= 3:
                    pe.wait_ge(ring_free, n - 2)
                return R[:, n % 3]

            pe.wait_ge(silu_b_ready, 1)
            pe.wait_ge(s_wm, 16)
            for b in range(B):
                for half in range(2):
                    r = claim("mod", b, half)
                    mm(r[:, 0:3 * D], silub[:, b], wm[:, 3 * half * D:3 * (half + 1) * D], start=True,
                       stop=True).then_inc(ring_full, 1)

            def transposes(key, src):
                r = claim(*key)
                for tt in range(TT):
                    last = nc.tensor.transpose(r[:, tt * P:(tt + 1) * P], src(tt), ident[:])
                last.then_inc(ring_full, 1)

            def prep_x(b):
                pe.wait_ge(hn_ready, b + 1)
                transposes(("h", b), lambda tt: hh[:, tt])
                transposes(("hn", b), lambda tt: hn[:, tt])

            def prep_qkv(b, tt):
                r = claim("qkv", b, tt)
                pe.wait_ge(ring_free, USE[("hn", b)] + 1)
                mm(r[:, 0:2 * D], xnT[:, tt], wqk[:].rearrange("p a d -> p (a d)"), start=True, stop=True)
                mm(r[:, 2 * D:3 * D], hT[:, tt], wvp[:], start=True, stop=True).then_inc(ring_full, 1)

            def prep_gate(b):
                pe.wait_ge(gqe_ready, b + 1)
                transposes(("gate", b), lambda tt: gqe[:, tt])
                r = claim("csum", b)
                for tt in range(TT):
                    last = mm(r[:, 0:1], gv[:, tt], ones[:], start=tt == 0, stop=tt == TT - 1)
                last.then_inc(ring_full, 1)

            def prep_operand(b, i):
                pe.wait_ge(lo_ready, b + 1)
                for name, a in (("q", 0), ("k", 1)):
                    transposes((name, b, i), lambda tt: ex[:, a, tt, 4 * i:4 * i + 4].rearrange(
                        "p h u v d -> p (h u v d)"))

            def scores(b, s):
                i, kt = s // TT, s % TT
                if kt == 0:
                    pe.wait_ge(ring_free, USE[("k", b, i)] + 1)
                for pr in range(2):
                    n = 2 * (STEPS * b + s) + pr
                    if n >= 2:
                        pe.wait_ge(tanh_ready, n - 1)
                    for u in range(2):
                        r0 = 32 * (2 * pr + u)
                        last = mm(S[:, pr, u], KA[r0:r0 + 32, i, kt * P:(kt + 1) * P], QA[r0:r0 + 32, i, :],
                                  start=True, stop=True)
                    last.then_inc(scores_ready, 1)

            def values(b, s):
                i, kt = s // TT, s % TT
                if s == 0 and b >= 1:
                    pe.wait_ge(fused_ready, b)
                if kt == 0:
                    pe.wait_ge(gvz_ready, QUADS * b + i + 1)
                for lane in range(LANES):
                    n = 2 * (STEPS * b + s) + lane // 2
                    pe.wait_ge(tanh_ready, n + 1)
                    last = mm(AV[32 * lane:32 * lane + 32, :], gvz[:, kt, i, lane], tanh[:, n % 4, lane % 2],
                              start=s == 0, stop=s == STEPS - 1)
                last.then_inc(av_done, 1)

            def post(b, part):
                if part == 0:
                    pe.wait_ge(fused_ready, b + 1)
                    r = claim("wo", b)
                    for tt in range(TT):
                        last = mm(r[:, tt * P:(tt + 1) * P], fT[:, tt * P:(tt + 1) * P], wo[:], start=True, stop=True)
                    last.then_inc(ring_full, 1)
                elif part == 1:
                    pe.wait_ge(h2_ready, b + 1)
                    transposes(("h2T", b), lambda tt: h2[:, tt])
                else:
                    r = claim("logit", b)
                    pe.wait_ge(ring_free, USE[("h2T", b)] + 1)
                    for tt in range(TT):
                        last = mm(r[:, tt * E:(tt + 1) * E], h2T[:, tt], ws[:], start=True, stop=True)
                    last.then_inc(ring_full, 1)

            pe.wait_ge(ident_ready, 1)
            prep_x(0)
            pe.wait_ge(wvp_ready, 1)
            for tt in range(TT):
                prep_qkv(0, tt)
            pe.wait_ge(consts_ready, 1)
            for i in range(QUADS):
                prep_operand(0, i)
            for b in range(B):
                more = b + 1 < B
                for s in range(STEPS):
                    scores(b, s)
                    if s > 0:
                        values(b, s - 1)
                    elif b > 0:
                        values(b - 1, STEPS - 1)
                    if s == 0 and more:
                        prep_x(b + 1)
                    if s == 1:
                        prep_gate(b)
                    if s in (2, 3) and more:
                        prep_qkv(b + 1, 2 * s - 4)
                        prep_qkv(b + 1, 2 * s - 3)
                    if b >= 1 and s in (5, 8, 9):
                        pe.wait_ge(s_wo, 16 * HEADS)
                        post(b - 1, (5, 8, 9).index(s))
                    if more and s in (12, 13, 14):
                        prep_operand(b + 1, s - 12)
                if more:
                    prep_operand(b + 1, QUADS - 1)
            values(B - 1, STEPS - 1)
            for part in range(3):
                post(B - 1, part)

            pe.wait_ge(h2l_ready, B)
            pe.wait_ge(tanh_ready, 2 * B * STEPS)
            pe.wait_ge(ring_free, len(order))
            pe.wait_ge(wlo, 3 * E)

            def up(n):
                t, e = n // E, n % E
                if n >= 2:
                    pe.wait_ge(hid_ready, n - 1)
                G, U = S[:, n % 2, 0, 0:F], S[:, n % 2, 1, 0:F]
                mm(G, h2h[:, t], wgh[:, e], start=True, stop=False)
                mm(G, h2h[:, t], wgl[:, e], start=False, stop=False)
                mm(U, h2h[:, t], wuh[:, e], start=True, stop=False)
                mm(U, h2h[:, t], wul[:, e], start=False, stop=False)
                mm(G, h2l[:, t], wgh[:, e], start=False, stop=True)
                mm(U, h2l[:, t], wuh[:, e], start=False, stop=True).then_inc(gu_ready, 1)

            def turn(n):
                pe.wait_ge(hid_ready, n + 1)
                if n >= 2:
                    pe.wait_ge(hTl_ready, n - 1)
                ps = (AV, R[:, 2])[n % 2]
                for k in range(FC):
                    last = nc.tensor.transpose(ps[:, k * P:(k + 1) * P], hid[:, n % 2, k * P:(k + 1) * P], ident[:])
                last.then_inc(hidT_ps, 1)

            def down(n):
                t, e = n // E, n % E
                pe.wait_ge(hTl_ready, n + 1)
                if e == 0 and t >= 2:
                    pe.wait_ge(yo_ready, t - 1)
                y = R[:, t % 2, 0:D]
                for k in range(FC):
                    rows = P if k < FC - 1 else FLAST
                    hi, lo = hTh[0:rows, n % 2, k], hTl[0:rows, n % 2, k]
                    mm(y, hi, wdh[0:rows, e, k], start=e == 0 and k == 0, stop=False)
                    mm(y, hi, wdl[0:rows, e, k], start=False, stop=False)
                    last = mm(y, lo, wdh[0:rows, e, k], start=False, stop=e == E - 1 and k == FC - 1)
                last.then_inc(down_done, 1)

            N = NT * E
            for n in range(N + 2):
                if n < N:
                    up(n)
                if 1 <= n <= N:
                    turn(n - 1)
                if n >= 2:
                    down(n - 2)


_INS = ["x", "w_q", "w_k", "w_v", "g_q", "g_k", "w_o", "b_o", "gamma", "beta"]
_FFN = ["Ws", "bs", "Wg", "Wu", "Wd"]


def kernel(**inputs):
    import numpy as np
    import concourse.bacc as bacc
    from concourse.bass_utils import run_bass_kernel_spmd

    nc = bacc.Bacc("TRN2", target_bir_lowering=False, num_devices=1)
    names = ["L0_attn_" + n for n in _INS] + ["L0_ffn_" + n for n in _FFN] + ["L0_c", "L0_wmod"]
    arrays, args = {}, []
    for name in names:
        a = np.ascontiguousarray(inputs[name])
        arrays[f"in_{name}"] = a
        args.append(nc.dram_tensor(f"in_{name}", a.shape, mybir.dt.from_np(a.dtype), kind="ExternalInput").ap())
    out = nc.dram_tensor("out_x", arrays["in_L0_attn_x"].shape, F32, kind="ExternalOutput").ap()
    adaln_block(nc, *args, out)
    r = run_bass_kernel_spmd(nc, [arrays], core_ids=[0])
    return r.results[0]["out_x"]
```

```python
from contextlib import ExitStack

import concourse.bass as bass
from concourse import mybir

ALU = mybir.AluOpType
ACT = mybir.ActivationFunctionType
AX_X = mybir.AxisListType.X
F32 = mybir.dt.float32
F32R = mybir.dt.float32r
I32 = mybir.dt.int32
U32 = mybir.dt.uint32
BF16 = mybir.dt.bfloat16

P = 128
HEADS = 16
QUADS = 4
LANES = 4
THRESHOLD = 0.27
SHARPNESS = 15.0
LN_EPS = 1e-5
NORM_EPS = 1e-12
RSQRT_MAGIC = 0x5F3759DF


def adaln_block(nc, x, w_q, w_k, w_v, g_q, g_k, w_o, b_o, gamma, beta, Ws, bs, Wg, Wu, Wd, c, wmod, out):
    B, T, D = x.shape
    HD = D // HEADS
    TT = T // P
    E, _, F = Wg.shape
    FC = -(-F // P)
    FLAST = F - (FC - 1) * P
    NT = B * TT
    TOP = 2
    NK = TOP * NT
    SLOTS = NK + E - 1
    GRING = 7
    AHEAD = GRING - 1
    STEPS = QUADS * TT
    POST_STEPS = (6, 8)
    GATE_STEP, TURN_STEP, OPERAND_STEPS = 8, 9, (12, 13, 14, 15)
    HEAT_FIRST = 20
    HEAT_STEPS = (0, 5, 6, 7, 8, 9, 10, 11, 12, 13, 14, 15)
    FIRST_STEPS = (1, 4, 5)
    MODS_FIRST = 4
    NG = 2 * HEADS
    PROJ = 3 * D + NG
    assert D == P and HD == 8 and T == TT * P and LANES * QUADS == HEADS and TT == 4

    ctx = ExitStack()
    with ctx:
        def sb(name, shape, dt=F32):
            return ctx.enter_context(nc.sbuf_tensor(name, shape, dt))

        def sem(name):
            return ctx.enter_context(nc.semaphore(name))

        tanh = sb("tanh", [P, 4, 2, T])
        wm = tanh[:, 0].rearrange("p a t -> p (a t)")[:, 0:6 * D]
        silub = tanh[:, 1].rearrange("p a t -> p (a t)")[:, 0:B * P].rearrange("p (b q) -> p b q", b=B)
        sg = tanh[:, 2, :, 0:F]
        hid = tanh[:, 3, :, 0:FC * P]
        ident = sb("ident", [P, P])
        ones = sb("ones", [P, 1])
        mhalf = sb("mhalf", [P, TT])
        warm = sb("warm", [P, 512], BF16)
        tanh_bias = sb("tanh_bias", [P, 1])
        wproj = sb("wproj", [P, PROJ])
        wqk = wproj[:, 0:2 * D]
        wgate = wproj[:, 2 * D:2 * D + NG]
        wvp = wproj[:, 2 * D + NG:PROJ]
        wv = sb("wv", [P, D])
        head32 = sb("head32", [P, 32])
        spread = sb("spread", [P, 4, P], F32R)
        wo = sb("wo", [P, D])
        ws = sb("ws", [P, E])
        bsb = sb("bsb", [P, E])
        gqk = sb("gqk", [P, 2, HD])
        gam = sb("gam", [P, 1])
        bet = sb("bet", [P, 1])
        bo = sb("bo", [P, D])
        cT = sb("cT", [P, B])
        siluc = sb("siluc", [P, B])
        mod = sb("mod", [P, B, 6, D])
        gab = sb("gab", [P, B, D])
        wgh = sb("wgh", [P, E, F], F32R)
        wgl = sb("wgl", [P, E, F], F32R)
        wuh = sb("wuh", [P, E, F], F32R)
        wul = sb("wul", [P, E, F], F32R)
        wdh = sb("wdh", [P, E, FC, D], F32R)
        wdl = sb("wdl", [P, E, FC, D], F32R)
        wraw = sb("wraw", [P, 2, FC * D])
        iota8 = sb("iota8", [P, E])
        xin = sb("xin", [P, B, TT, D])
        x1 = xin
        h2T = sb("h2T", [P, TT, D])
        lg = sb("lg", [P, NT, E])
        h2rows = nc.dram_tensor("h2rows", (NT * P, D), F32, kind="Internal").ap()
        yrows = nc.dram_tensor("yrows", ((NK + SLOTS) * P, D), F32, kind="Internal").ap()
        st = sb("st", [P, TT, 6])
        mv = sb("mv", [P, TT, 2])
        ve = sb("ve", [P, TT])
        rstd = sb("rstd", [P, TT])
        room = sb("room", [P, 4, TT * D])
        hh, hn, hT, xnT = (room[:, n].rearrange("p (t d) -> p t d", t=TT) for n in range(4))
        qkT_hi = sb("qkT_hi", [P, 2, TT * P], F32R)
        qkT_lo = sb("qkT_lo", [P, 2, TT * P], F32R)
        spread_f = room[:, 3].rearrange("p (k q) -> p k q", q=P)
        proj = sb("proj", [P, TT, PROJ])
        sq = sb("sq", [P, TT, 2 * D])
        ss = sb("ss", [P, TT * NG])
        yr = sb("yr", [P, TT * NG])
        yt = sb("yt", [P, TT * NG])
        dots = sb("dots", [P, TT, NG])
        gt = sb("gt", [P, TT, NG])
        gate = sb("gate", [P, TT, NG])
        gqe = sb("gqe", [P, TT, D])
        gv = sb("gv", [P, TT, D])
        gvz = sb("gvz", [P, TT, QUADS, LANES, 32])
        QA = sb("QA", [P, QUADS, TT * P], F32R)
        KA = sb("KA", [P, QUADS, TT * P], F32R)
        GQT = sb("GQT", [P, TT * P])
        Cs = sb("Cs", [P, 1])
        fT = sb("fT", [P, TT * P])
        xb = sb("xb", [P, TT, D])
        st2 = sb("st2", [P, TT, 6])
        mv2 = sb("mv2", [P, TT, 2])
        ve2 = sb("ve2", [P, TT])
        rstd2 = sb("rstd2", [P, TT])
        h2 = sb("h2", [P, TT, D])
        tri = sb("tri", [P, P], BF16)
        onesq = sb("onesq", [P, P], BF16)
        iotap = sb("iotap", [P, P], BF16)
        iotas = sb("iotas", [P, SLOTS])
        part1 = sb("part1", [P, 1])
        knum = sb("knum", [P, 2, NK])
        spare = sb("spare", [P, SLOTS])
        top = sb("top", [P, NT, 8])
        topi = sb("topi", [P, NT, 8], U32)
        topf = sb("topf", [P, NT, 8])
        dl = sb("dl", [P, NT])
        th = sb("th", [P, NT])
        w12 = sb("w12", [P, TOP, NT])
        oh = sb("oh", [P, TOP, NT, E])
        pick = sb("pick", [P, NT, E], BF16)
        before = sb("before", [P, NT + 1, E], BF16)
        tot = sb("tot", [P, 4, E])
        toti = sb("toti", [P, E], I32)
        tend = sb("tend", [P, E])
        tbase = sb("tbase", [P, E])
        slot3 = sb("slot3", [P, NT, E])
        slotm = sb("slotm", [P, TOP, NT, E])
        slot = sb("slot", [P, NK])
        sloti = sb("sloti", [P, 3, NK], I32)
        slotf = sb("slotf", [P, 2, NK])
        lo1h = gvz[:].rearrange("p t i j e -> p (t i j e)").bitcast(BF16)[:, 0:NK * P].rearrange(
            "p (n q) -> p n q", q=P)
        hi1h = room[:].rearrange("p a q -> p (a q)").bitcast(BF16)[:, 0:NK * 3 * SLOTS].rearrange(
            "p (n a j) -> p n a j", n=NK, a=3)
        eotc = sb("eotc", [P, SLOTS, E])
        eotf = sb("eotf", [P, SLOTS])
        eot = sb("eot", [P, SLOTS], I32)
        inv = sb("inv", [P, 4, SLOTS])
        gidx = sb("gidx", [P, SLOTS], I32)
        sidx = sb("sidx", [P, SLOTS], I32)
        xg = sb("xg", [P, GRING, D])
        yv = sb("yv", [P, GRING, D])
        turned_hi = QA[:, 0:3].rearrange("p a (k q) -> p a k q", k=FC + 1)
        turned_lo = KA[:, 0:3].rearrange("p a (k q) -> p a k q", k=FC + 1)
        y12 = (room[:].rearrange("p a (t d) -> p (a t) d", d=D),
               gvz[:].rearrange("p t i j e -> p (t i j e)").rearrange("p (n d) -> p n d", d=D))

        S = ctx.enter_context(nc.psum_tensor("S", [P, 2, 2, 512], F32))
        AV = ctx.enter_context(nc.psum_tensor("AV", [P, 512], F32))
        R = ctx.enter_context(nc.psum_tensor("R", [P, 3, 512], F32))

        s_c, s_wm, s_wqkv, s_small, s_bo = sem("s_c"), sem("s_wm"), sem("s_wqkv"), sem("s_small"), sem("s_bo")
        s_x = [sem(f"s_x{b}") for b in range(B)]
        s_wo = sem("s_wo")
        s_raw = [sem("s_raw0"), sem("s_raw1")]
        out_stored = sem("out_stored")
        ident_ready = sem("ident_ready")
        consts_ready = sem("consts_ready")
        warm_ready = sem("warm_ready")
        silu_c_ready = sem("silu_c_ready")
        silu_b_ready = sem("silu_b_ready")
        mod_copied = sem("mod_copied")
        mod_ready = sem("mod_ready")
        spread_ready = sem("spread_ready")
        wgate_ready = sem("wgate_ready")
        wvp_ready = sem("wvp_ready")
        gab_ready = sem("gab_ready")
        dve_chain = sem("dve_chain")
        pool_chain = sem("pool_chain")
        var_ready = sem("var_ready")
        rstd_ready = sem("rstd_ready")
        hn_ready = sem("hn_ready")
        xT_ready = sem("xT_ready")
        qkv_ready = sem("qkv_ready")
        sq_ready = sem("sq_ready")
        rn_ready = sem("rn_ready")
        qn_ready = sem("qn_ready")
        hi_ready = sem("hi_ready")
        lo_ready = sem("lo_ready")
        dots_ready = sem("dots_ready")
        gt_ready = sem("gt_ready")
        gate_ready = sem("gate_ready")
        gv_ready = sem("gv_ready")
        gqe_ready = sem("gqe_ready")
        gvz_ready = sem("gvz_ready")
        ring_full = sem("ring_full")
        ring_free = sem("ring_free")
        ring_free_act = sem("ring_free_act")
        scores_ready = sem("scores_ready")
        tanh_ready = sem("tanh_ready")
        av_done = sem("av_done")
        fused_ready = sem("fused_ready")
        xb_ready = sem("xb_ready")
        var2_ready = sem("var2_ready")
        rstd2_ready = sem("rstd2_ready")
        h2_ready = sem("h2_ready")
        h2_stored = sem("h2_stored")
        route_in = sem("route_in")
        rank_ready = sem("rank_ready")
        onehot_ready = sem("onehot_ready")
        inv_ready = sem("inv_ready")
        idx_ready = sem("idx_ready")
        gathered = [sem(f"gathered{i}") for i in range(GRING)]
        scattered = [sem(f"scattered{i}") for i in range(GRING)]
        turn_done = sem("turn_done")
        turned_hi_ready = sem("turned_hi_ready")
        turned_lo_ready = sem("turned_lo_ready")
        y_loaded = [sem(f"y_loaded{b}") for b in range(B)]
        y1_ready = sem("y1_ready")
        mix_ready = sem("mix_ready")
        split_ready = sem("split_ready")
        wsplit = sem("wsplit")
        wlo = sem("wlo")
        dl_ready = sem("dl_ready")
        th_ready = sem("th_ready")
        gu_ready = sem("gu_ready")
        silu_ready = sem("silu_ready")
        hid_ready = sem("hid_ready")
        down_done = sem("down_done")
        y_ready = sem("y_ready")
        yo_ready = sem("yo_ready")

        TURNS = range(-3, SLOTS)

        def turn_parts(m):
            return 0 if m >= 0 else FC, FC + 1 if m + 3 < SLOTS else FC

        def turn_bank(m):
            k0, k1 = turn_parts(m)
            return (AV[:], R[:, 2])[m % 2][:, k0 * P:k1 * P].rearrange("p (k q) -> p k q", q=P)

        assert F <= FC * P and (FC + 1) * P == 512

        xs = x.rearrange("b (p t) d -> p b t d", t=TT)
        outs = out.rearrange("b (p t) d -> p b t d", t=TT)
        NW = 2 * E

        block = ctx.enter_context(nc.Block())

        USE = {}
        order = []

        def use(*key):
            USE[key] = len(order)
            order.append(key)

        def by_scalar(key):
            return key[0] == "q" or key[0:2] == ("qkv", 0) or (key[0] == "mod" and key[1:] != (0, 0))

        def freed(*key):
            mine = by_scalar(key)
            count = sum(1 for k in order[:USE[key] + 1] if by_scalar(k) == mine)
            return (ring_free_act if mine else ring_free), count

        def operand_uses(b, i):
            use("q", b, i)
            use("k", b, i)

        for n in range(2 * B):
            use("mod", n // 2, n % 2)
            if n == MODS_FIRST - 1:
                use("h", 0)
                use("hn", 0)
        for tt in range(TT):
            use("qkv", 0, tt)
        use("qT", 0)
        use("kT", 0)
        operand_uses(0, 0)
        for b in range(B):
            more = b + 1 < B
            if more:
                use("h", b + 1)
                use("hn", b + 1)
                use("qkv", b + 1, 0)
            if b == 0:
                operand_uses(0, 1)
            if b >= 1:
                use("wo", b - 1)
            if more:
                for tt in range(1, TT):
                    use("qkv", b + 1, tt)
            if b == 0:
                operand_uses(0, 2)
            use("gate", b)
            use("csum", b)
            if b == 0:
                operand_uses(0, 3)
            if b >= 1:
                use("h2T", b - 1)
                use("logit", b - 1)
            if more:
                use("qT", b + 1)
                use("kT", b + 1)
                for i in range(QUADS):
                    operand_uses(b + 1, i)
        use("wo", B - 1)
        use("h2T", B - 1)
        use("logit", B - 1)

        @block.sync
        def _(sp):
            sp.dma_start(wm[:], wmod).then_inc(s_wm, 16)
            sp.dma_start(xin[:, 0], xs[:, 0]).then_inc(s_x[0], 16)
            sp.dma_start(wqk[:, 0:D], w_q).then_inc(s_wqkv, 16)
            sp.dma_start(wqk[:, D:2 * D], w_k).then_inc(s_wqkv, 16)
            sp.dma_start(wv[:], w_v).then_inc(s_wqkv, 16)
            for lane in range(LANES):
                src = w_o.rearrange("(i j d) n -> j i d n", i=QUADS, j=LANES)[lane]
                for i in range(QUADS):
                    r0 = 32 * lane + HD * i
                    sp.dma_start(wo[r0:r0 + HD, :], src[i]).then_inc(s_wo, 16)
            for b in range(1, B):
                sp.dma_start(xin[:, b], xs[:, b]).then_inc(s_x[b], 16)
            sp.dma_start(bo[:], b_o.partition_broadcast(P)).then_inc(s_bo, 16)
            sp.wait_ge(consts_ready, 1)
            for n in range(3 * E):
                if n >= 2:
                    sp.wait_ge(wlo, n - 1)
                if n < NW:
                    W = Wg if n < E else Wu
                    sp.dma_start(wraw[:, n % 2, 0:F], W[n % E]).then_inc(s_raw[n % 2], 16)
                else:
                    e = n - NW
                    sp.dma_start(wraw[:, n % 2, 0:(FC - 1) * D],
                                 Wd[e, 0:(FC - 1) * P].rearrange("(k p) d -> p k d", p=P)).then_inc(s_raw[n % 2], 16)
                    sp.dma_start(wraw[0:FLAST, n % 2, (FC - 1) * D:FC * D],
                                 Wd[e, (FC - 1) * P:F]).then_inc(s_raw[n % 2], 16)
            yr_v = yrows[0:NK * P].rearrange("(k b t p) d -> b k p t d", k=TOP, b=B, t=TT)
            for i in range(GRING):
                sp.wait_ge(scattered[i], 16 * len(range(i, SLOTS, GRING)))
            for b in range(B):
                for k in range(TOP):
                    sp.dma_start(y12[k][:, TT * b:TT * (b + 1)], yr_v[b, k]).then_inc(y_loaded[b], 16)
            for b in range(B):
                sp.wait_ge(yo_ready, b + 1)
                sp.dma_start(outs[:, b], x1[:, b]).then_inc(out_stored, 16)
            sp.wait_ge(out_stored, 16 * B)

        @block.gpsimd
        def _(pool):
            g = nc.gpsimd
            chain = [0]

            def link(ins):
                chain[0] += 1
                ins.then_inc(pool_chain, 1)
                pool.wait_ge(pool_chain, chain[0])

            link(g.memset(ident[:], 0.0))
            g.affine_select(out=ident[:], in_=ident[:], compare_op=ALU.not_equal, fill=1.0, base=0,
                            pattern=[[-1, P]], channel_multiplier=1).then_inc(ident_ready, 1)
            g.memset(mhalf[:], -0.5)
            g.memset(warm[:], 1.0).then_inc(warm_ready, 1)
            g.memset(gvz[:], 0.0)
            g.memset(wraw[:], 0.0)
            g.memset(tanh_bias[:], -THRESHOLD * SHARPNESS)
            g.memset(ones[:], 1.0)
            g.memset(onesq[:], 1.0)
            g.memset(before[:, 0], 0.0)
            link(g.memset(tri[:], 1.0))
            g.affine_select(out=tri[:], in_=tri[:], compare_op=ALU.is_gt, fill=0.0, base=0,
                            pattern=[[1, P]], channel_multiplier=-1)
            g.iota(iotap[:], [[1, P]], base=0, channel_multiplier=0, allow_small_or_imprecise_dtypes=True)
            g.iota(iotas[:], [[1, SLOTS]], base=0, channel_multiplier=0, allow_small_or_imprecise_dtypes=True)
            g.iota(part1[:], [[0, 1]], base=1, channel_multiplier=1, allow_small_or_imprecise_dtypes=True)
            g.iota(spare[:], [[P, SLOTS]], base=NK * P + 1, channel_multiplier=1,
                   allow_small_or_imprecise_dtypes=True)
            g.iota(knum[:, 0], [[0, TOP], [1, NT]], base=0, channel_multiplier=0,
                   allow_small_or_imprecise_dtypes=True)
            g.iota(knum[:, 1], [[NT, TOP], [0, NT]], base=0, channel_multiplier=0,
                   allow_small_or_imprecise_dtypes=True)
            g.iota(iota8[:], [[1, E]], base=0, channel_multiplier=0,
                   allow_small_or_imprecise_dtypes=True).then_inc(consts_ready, 1)
            pool.wait_ge(s_wqkv, 48)
            g.tensor_copy(wvp.rearrange("p (j i d) -> p i j d", j=LANES, i=QUADS),
                          wv[:].rearrange("p (i j d) -> p i j d", i=QUADS, j=LANES)).then_inc(wvp_ready, 1)

            def power(dst, src, ready, n):
                pool.wait_ge(ready, n)
                return g.tensor_tensor(dst, src, mhalf[:], ALU.pow)

            def weights(n):
                pool.wait_ge(wsplit, n + 1)
                if n < NW:
                    hi, lo = ((wgh, wgl), (wuh, wul))[n // E]
                    e = n % E
                    g.tensor_tensor(lo[:, e], wraw[:, n % 2, 0:F], hi[:, e].bitcast(F32),
                                    ALU.subtract).then_inc(wlo, 1)
                else:
                    e = n - NW
                    g.tensor_tensor(wdl[:, e].rearrange("p k d -> p (k d)"), wraw[:, n % 2],
                                    wdh[:, e].rearrange("p k d -> p (k d)").bitcast(F32),
                                    ALU.subtract).then_inc(wlo, 1)

            def norm(b, which):
                power(rstd[:], ve[:], var_ready, 2 * b + which + 1).then_inc(rstd_ready, 1)

            def squares(b, half):
                t0, t1 = half * TT // 2, (half + 1) * TT // 2
                pool.wait_ge(*freed("qkv", b, t1 - 1))
                if b >= 1:
                    pool.wait_ge(rn_ready, b)
                g.tensor_tensor(sq[:, t0:t1], proj[:, t0:t1, 0:2 * D], proj[:, t0:t1, 0:2 * D],
                                ALU.mult).then_inc(sq_ready, 1)

            def unit_qk(b):
                pool.wait_ge(rn_ready, b + 1)
                q = proj[:, :, 0:2 * D].rearrange("p t (g d) -> p t g d", d=HD)
                g.tensor_tensor(q, q, yr[:].rearrange("p (t g) -> p t g", t=TT).unsqueeze(3).to_broadcast(
                    [P, TT, NG, HD]), ALU.mult).then_inc(qn_ready, 1)

            def gated(b):
                pool.wait_ge(gate_ready, b + 1)
                if b >= 1:
                    pool.wait_ge(ring_full, USE[("csum", b - 1)] + 1)
                    pool.wait_ge(gvz_ready, QUADS * b)
                for tt in range(TT):
                    gk = gate[:, tt, HEADS:NG].rearrange("p (i j) -> p j i", j=LANES)
                    last = g.tensor_tensor(gv[:, tt].rearrange("p (j i d) -> p j i d", j=LANES, d=HD),
                                           proj[:, tt, 2 * D + NG:PROJ].rearrange(
                                               "p (j i d) -> p j i d", j=LANES, d=HD),
                                           gk.unsqueeze(3).to_broadcast([P, LANES, QUADS, HD]), ALU.mult)
                last.then_inc(gv_ready, 1)
                for tt in range(TT):
                    gq = gate[:, tt, 0:HEADS].rearrange("p (i j) -> p j i", j=LANES)
                    last = g.tensor_copy(gqe[:, tt].rearrange("p (j i d) -> p j i d", j=LANES, d=HD),
                                         gq.unsqueeze(3).to_broadcast([P, LANES, QUADS, HD]))
                last.then_inc(gqe_ready, 1)

            def residual(b):
                if b >= 1:
                    pool.wait_ge(var2_ready, b)
                g.tensor_tensor(xb[:], xin[:, b], gab[:, b].unsqueeze(1).to_broadcast([P, TT, D]),
                                ALU.add).then_inc(xb_ready, 1)

            def store_h2(b):
                pool.wait_ge(h2_ready, b + 1)
                pool.dma_start(h2rows[TT * P * b:TT * P * (b + 1)].rearrange("(t p) d -> p t d", p=P),
                               h2[:]).then_inc(h2_stored, 16)

            def norm2(b):
                power(rstd2[:], ve2[:], var2_ready, b + 1).then_inc(rstd2_ready, 1)

            norm(0, 0)
            norm(0, 1)
            norm(1, 0)
            norm(1, 1)
            gated(0)
            for b in range(B):
                more = b + 1 < B
                n = 3 * E // B * b
                if b >= 1:
                    residual(b - 1)
                weights(n)
                if b >= 1:
                    norm2(b - 1)
                if more:
                    squares(b + 1, 0)
                    squares(b + 1, 1)
                if b >= 1:
                    store_h2(b - 1)
                weights(n + 1)
                if more:
                    unit_qk(b + 1)
                if b + 2 < B:
                    norm(b + 2, 0)
                weights(n + 2)
                if more:
                    gated(b + 1)
                if b + 2 < B:
                    norm(b + 2, 1)
                weights(n + 3)
                if b == 0:
                    pool.wait_ge(mod_ready, 2)
                    pool.wait_ge(s_bo, 16)
                    g.tensor_tensor(gab[:], mod[:, :, 2], bo[:].unsqueeze(1).to_broadcast([P, B, D]),
                                    ALU.mult).then_inc(gab_ready, 1)
                    pool.wait_ge(gab_ready, 1)
                weights(n + 4)
                weights(n + 5)
            residual(B - 1)
            norm2(B - 1)
            store_h2(B - 1)

            pool.wait_ge(h2_stored, 16 * B)
            pool.wait_ge(idx_ready, 2)

            def gather(j):
                if j >= GRING:
                    pool.wait_ge(turn_done, j - GRING + 1)
                pool.indirect_dma_start(xg[:, j % GRING], None, h2rows,
                                        bass.IndirectOffsetOnAxis(ap=gidx[:, j:j + 1], axis=0)
                                        ).then_inc(gathered[j % GRING], 16)

            for j in range(AHEAD):
                gather(j)
            for j in range(SLOTS):
                if j + AHEAD < SLOTS:
                    gather(j + AHEAD)
                pool.wait_ge(y_ready, j + 1)
                pool.indirect_dma_start(yrows, bass.IndirectOffsetOnAxis(ap=sidx[:, j:j + 1], axis=0),
                                        yv[:, j % GRING], None).then_inc(scattered[j % GRING], 16)

        @block.scalar
        def _(act):
            a = nc.scalar
            with nc.allow_non_contiguous_dma(reason="small transposed and column loads"):
                act.dma_start(cT[:], c.rearrange("b d -> d b")).then_inc(s_c, 16)
                act.dma_start(gam[:], gamma.rearrange("(d a) -> d a", a=1)).then_inc(s_small, 16)
                act.dma_start(bet[:], beta.rearrange("(d a) -> d a", a=1)).then_inc(s_small, 16)
            act.dma_start(gqk[:, 0], g_q.partition_broadcast(P)).then_inc(s_small, 16)
            act.dma_start(gqk[:, 1], g_k.partition_broadcast(P)).then_inc(s_small, 16)
            act.dma_start(ws[:], Ws).then_inc(s_small, 16)
            act.dma_start(bsb[:], bs.partition_broadcast(P)).then_inc(s_small, 16)
            act.wait_ge(warm_ready, 1)
            a.activation(gt[:, 0, 0:1], warm[:, 0:1], ACT.Silu)
            act.wait_ge(s_c, 16)
            a.activation(siluc[:], cT[:], ACT.Silu).then_inc(silu_c_ready, 1)

            def gates(b):
                act.wait_ge(dots_ready, b + 1)
                if b >= 1:
                    act.wait_ge(gate_ready, b)
                a.activation(gt[:], dots[:], ACT.Tanh, scale=0.5).then_inc(gt_ready, 1)

            def full(*key):
                act.wait_ge(ring_full, USE[key] + 1)
                return R[:, USE[key] % 3]

            def turned_qk(b):
                for a, name in enumerate(("qT", "kT")):
                    r = full(name, b)
                    if b >= 1:
                        act.wait_ge(ring_full, USE[("k", b - 1, QUADS - 1)] + 1)
                    if b == 0:
                        act.wait_ge(spread_ready, 1)
                    a_hi = qkT_hi[:, a]
                    nc.scalar.activation(a_hi, r[:], ACT.Copy).then_inc(hi_ready, 1)

            def operand(b, i):
                r = full("q", b, i)
                if b >= 1:
                    act.wait_ge(scores_ready, 2 * (STEPS * (b - 1) + TT * (i + 1)))
                a.activation(QA[:, i], r[:], ACT.Copy).then_inc(ring_free_act, 1)

            for b in range(B):
                for half in range(2):
                    if (b, half) != (0, 0):
                        r = full("mod", b, half)
                        for n in range(3):
                            last = a.activation(mod[:, b, 3 * half + n], r[:, n * D:(n + 1) * D], ACT.Copy,
                                                bias=1.0 if n == 1 else 0.0)
                        last.then_inc(ring_free_act, 1)
            for tt in range(TT):
                if tt == 0:
                    act.wait_ge(wgate_ready, 1)
                r = full("qkv", 0, tt)
                a.activation(sq[:, tt], r[:, 0:2 * D], ACT.Square).then_inc(sq_ready, 1)
                a.activation(proj[:, tt], r[:, 0:PROJ], ACT.Copy).then_inc(ring_free_act, 1)
            gates(0)
            turned_qk(0)
            operand(0, 0)
            act.wait_ge(consts_ready, 1)
            for b in range(B):
                more = b + 1 < B
                for s in range(STEPS):
                    for pr in range(2):
                        n = 2 * (STEPS * b + s) + pr
                        act.wait_ge(scores_ready, n + 1)
                        if n >= 4:
                            act.wait_ge(av_done, (n - 4) // 2 + 1)
                        a.activation(tanh[:, n % 4], S[:, pr], ACT.Tanh, bias=tanh_bias[:, 0:1],
                                     scale=SHARPNESS).then_inc(tanh_ready, 1)
                    if b == 0 and s in FIRST_STEPS:
                        operand(0, 1 + FIRST_STEPS.index(s))
                    if s == GATE_STEP and more:
                        gates(b + 1)
                    if s == TURN_STEP and more:
                        turned_qk(b + 1)
                    if s in OPERAND_STEPS and more:
                        operand(b + 1, OPERAND_STEPS.index(s))
            act.wait_ge(dl_ready, 1)
            a.activation(th[:], dl[:], ACT.Tanh, scale=0.5).then_inc(th_ready, 1)

            def turn_hi(m):
                k0, k1 = turn_parts(m)
                act.wait_ge(turn_done, m + 4)
                a.activation(turned_hi[:, m % 3, k0:k1], turn_bank(m), ACT.Copy).then_inc(turned_hi_ready, 1)

            turn_hi(-3)
            turn_hi(-2)
            for j in range(SLOTS + 1):
                if j < SLOTS:
                    act.wait_ge(gu_ready, j + 1)
                    if j >= 2:
                        act.wait_ge(hid_ready, j - 1)
                    a.activation(sg[:, j % 2], S[:, j % 2, 0, 0:F], ACT.Silu).then_inc(silu_ready, 1)
                turn_hi(j - 1)
            for b in range(B):
                act.wait_ge(y_loaded[b], 16 * TOP)
                for tt in range(TT):
                    n = TT * b + tt
                    last = a.activation(y12[0][:, n], y12[0][:, n], ACT.Copy, scale=w12[:, 0, n:n + 1])
                last.then_inc(y1_ready, 1)

        @block.vector
        def _(dve):
            v = nc.vector
            chain = [0]

            def link(ins):
                chain[0] += 1
                ins.then_inc(dve_chain, 1)
                dve.wait_ge(dve_chain, chain[0])

            def full(*key):
                dve.wait_ge(ring_full, USE[key] + 1)
                return R[:, USE[key] % 3]

            dve.wait_ge(ident_ready, 1)
            v.memset(spread_f, 0.0)
            link(v.tensor_reduce(head32[:], ident[:].rearrange("p (i r) -> p r i", i=QUADS), AX_X, ALU.add))
            h4 = head32[:].rearrange("p (j d) -> p j d", d=HD).unsqueeze(2).to_broadcast([P, LANES, 2, HD])
            for k in range(2):
                v.tensor_copy(spread_f[:, k].rearrange("p (j u w d) -> p j u w d", j=LANES, u=2, w=2)[:, :, k], h4)
                last = v.tensor_copy(spread_f[:, 2 + k].rearrange(
                    "p (j u w d) -> p j u w d", j=LANES, u=2, w=2)[:, :, :, k], h4)
            link(last)
            v.tensor_copy(spread[:], spread_f).then_inc(spread_ready, 1)
            dve.wait_ge(silu_c_ready, 1)
            v.tensor_copy(silub, siluc[:].unsqueeze(2).to_broadcast([P, B, P])).then_inc(silu_b_ready, 1)
            dve.wait_ge(s_wqkv, 48)
            dve.wait_ge(s_small, 96)
            link(v.tensor_tensor(sq[:, 0].rearrange("p (a h d) -> p a h d", a=2, h=HEADS),
                                 wqk.rearrange("p (a h d) -> p a h d", a=2, h=HEADS),
                                 gqk[:].unsqueeze(2).to_broadcast([P, 2, HEADS, HD]), ALU.mult))
            v.tensor_reduce(wgate, sq[:, 0].rearrange("p (g d) -> p g d", d=HD), AX_X, ALU.add
                            ).then_inc(wgate_ready, 1)

            def mod_first():
                r = full("mod", 0, 0)
                v.tensor_copy(mod[:, 0, 0], r[:, 0:D])
                v.tensor_copy(mod[:, 0, 2], r[:, 2 * D:3 * D])
                v.tensor_scalar(mod[:, 0, 1], r[:, D:2 * D], 1.0, None, ALU.add).then_inc(ring_free, 1)
                dve.wait_ge(ring_free, 1)

            def mod_gates(half):
                m = mod[:, :, 3 * half + 2]
                dve.wait_ge(*freed("mod", B - 1, 1))
                if half == 1:
                    dve.wait_ge(mod_ready, 1)
                v.tensor_scalar(h2[:], m, 0.0, 0.5, ALU.is_ge, ALU.subtract)
                link(v.scalar_tensor_tensor(h2T[:], m, -1.0, m, ALU.mult, ALU.max))
                link(v.tensor_scalar(h2T[:], h2T[:], 0.25, 2.0, ALU.max, ALU.mult))
                v.tensor_tensor(m, h2[:], h2T[:], ALU.mult).then_inc(mod_ready, 1)

            def stats(src, st, mv, ve, var_sem):
                for tt in range(TT):
                    last = v.bn_stats(st[:, tt], src[:, tt])
                link(last)
                for tt in range(TT):
                    last = v.bn_aggr(mv[:, tt], st[:, tt])
                link(last)
                v.tensor_scalar(ve[:], mv[:, :, 1], LN_EPS, None, ALU.add).then_inc(var_sem, 1)

            def normalize(dst, src, mv, rstd, ready, n):
                dve.wait_ge(ready, n)
                for tt in range(TT):
                    last = v.tensor_scalar(dst[:, tt], src[:, tt], mv[:, tt, 0:1], rstd[:, tt:tt + 1],
                                           ALU.subtract, ALU.mult)
                return last

            def norms_center(b):
                dve.wait_ge(s_x[b], 16)
                stats(xin[:, b], st, mv, ve, var_ready)
                if b == 0:
                    mod_first()
                else:
                    dve.wait_ge(ring_full, USE[("hn", b - 1)] + 1)
                    dve.wait_ge(*freed("mod", b, 0))
                for tt in range(TT):
                    last = v.scalar_tensor_tensor(hh[:, tt], xin[:, b, tt], mv[:, tt, 0:1], mod[:, b, 1],
                                                  ALU.subtract, ALU.mult)
                link(last)

            def norms_h(b):
                dve.wait_ge(rstd_ready, 2 * b + 1)
                for tt in range(TT):
                    last = v.scalar_tensor_tensor(hh[:, tt], hh[:, tt], rstd[:, tt:tt + 1], mod[:, b, 0],
                                                  ALU.mult, ALU.add)
                link(last)
                stats(hh, st, mv, ve, var_ready)

            def norms_hn(b):
                normalize(hn, hh, mv, rstd, rstd_ready, 2 * b + 2).then_inc(hn_ready, 1)

            def prep_xT(b):
                r = full("h", b)
                if b >= 1:
                    dve.wait_ge(ring_full, USE[("qkv", b - 1, TT - 1)] + 1)
                v.tensor_copy(hT.rearrange("p t d -> p (t d)"), r[:]).then_inc(ring_free, 1)
                r = full("hn", b)
                v.tensor_scalar(xnT.rearrange("p t d -> p (t d)"), r[:], gam[:, 0:1], bet[:, 0:1], ALU.mult,
                                ALU.add).then_inc(ring_free, 1)

            def prep_qkv(b, tt):
                if b >= 1:
                    dve.wait_ge(gv_ready, b)
                    dve.wait_ge(ring_full, USE[("kT", b - 1)] + 1)
                r = full("qkv", b, tt)
                v.tensor_copy(proj[:, tt], r[:, 0:PROJ]).then_inc(ring_free, 1)

            def prep_rn(b):
                dve.wait_ge(sq_ready, TT + 2 * b)
                link(v.tensor_reduce(ss[:], sq[:].rearrange("p t (g d) -> p (t g) d", d=HD), AX_X, ALU.add))
                link(v.tensor_scalar(ss[:], ss[:], NORM_EPS * NORM_EPS, None, ALU.max))
                link(v.tensor_scalar(yt[:].bitcast(I32), ss[:].bitcast(I32), 1, None, ALU.arith_shift_right))
                if b >= 2:
                    dve.wait_ge(qn_ready, b - 1)
                v.tensor_scalar(yr[:].bitcast(I32), yt[:].bitcast(I32), -1.0, float(RSQRT_MAGIC),
                                ALU.mult, ALU.add)
                link(v.tensor_scalar(ss[:], ss[:], -0.5, None, ALU.mult))
                for it in range(3):
                    link(v.tensor_tensor(yt[:], yr[:], yr[:], ALU.mult))
                    link(v.tensor_tensor(yt[:], yt[:], ss[:], ALU.mult))
                    last = v.scalar_tensor_tensor(yr[:], yt[:], 1.5, yr[:], ALU.add, ALU.mult)
                    if it < 2:
                        link(last)
                last.then_inc(rn_ready, 1)
                dve.wait_ge(rn_ready, b + 1)

            def prep_dots(b):
                dve.wait_ge(*freed("qkv", b, TT - 1))
                if b >= 1:
                    dve.wait_ge(gt_ready, b)
                v.tensor_tensor(dots[:], proj[:, :, 2 * D:2 * D + NG], yr[:].rearrange("p (t g) -> p t g", t=TT),
                                ALU.mult).then_inc(dots_ready, 1)

            def prep_lo(b):
                for a, name in enumerate(("qT", "kT")):
                    dve.wait_ge(hi_ready, 2 * b + a + 1)
                    r = full(name, b)
                    v.tensor_tensor(qkT_lo[:, a], r[:], qkT_hi[:, a].bitcast(F32), ALU.subtract
                                    ).then_inc(ring_free, 1)

            def value_operand(b, i):
                dve.wait_ge(gv_ready, b + 1)
                if b >= 1:
                    dve.wait_ge(av_done, STEPS * (b - 1) + TT * (i + 1))
                v.tensor_copy(gvz[:, :, i, :, HD * i:HD * (i + 1)],
                              gv[:].rearrange("p t (j i d) -> p t j i d", j=LANES, d=HD)[:, :, :, i]
                              ).then_inc(gvz_ready, 1)

            def prep_gates(b):
                dve.wait_ge(gt_ready, b + 1)
                if b >= 1:
                    dve.wait_ge(gqe_ready, b)
                v.tensor_scalar(gate[:, :, 0:HEADS], gt[:, :, 0:HEADS], 0.375, 0.625, ALU.mult, ALU.add)
                v.tensor_scalar(gate[:, :, HEADS:NG], gt[:, :, HEADS:NG], 0.1875, 0.3125, ALU.mult, ALU.add
                                ).then_inc(gate_ready, 1)

            def prep_gqt(b):
                r = full("gate", b)
                v.tensor_copy(GQT[:], r[:]).then_inc(ring_free, 1)
                r = full("csum", b)
                v.tensor_copy(Cs[:], r[:, 0:1]).then_inc(ring_free, 1)

            def prep_operands(b, i):
                if b >= 1:
                    dve.wait_ge(scores_ready, 2 * (STEPS * (b - 1) + TT * (i + 1)))
                r = full("k", b, i)
                v.tensor_copy(KA[:, i], r[:]).then_inc(ring_free, 1)

            def fuse(b):
                dve.wait_ge(av_done, STEPS * (b + 1))
                if b >= 1:
                    dve.wait_ge(ring_full, USE[("wo", b - 1)] + 1)
                dve.wait_ge(*freed("csum", b))
                v.scalar_tensor_tensor(fT[:], AV[:], Cs[:, 0:1], GQT[:], ALU.add, ALU.mult).then_inc(fused_ready, 1)

            def post_x1(b):
                r = full("wo", b)
                dve.wait_ge(xb_ready, b + 1)
                v.tensor_tensor(x1[:, b], r[:].rearrange("p (t d) -> p t d", t=TT),
                                mod[:, b, 2].unsqueeze(1).to_broadcast([P, TT, D]), ALU.mult).then_inc(ring_free, 1)
                dve.wait_ge(*freed("wo", b))
                link(v.tensor_tensor(x1[:, b], x1[:, b], xb[:], ALU.add))
                stats(x1[:, b], st2, mv2, ve2, var2_ready)

            def post_center(b):
                if b >= 1:
                    dve.wait_ge(ring_full, USE[("h2T", b - 1)] + 1)
                    dve.wait_ge(h2_stored, 16 * b)
                for tt in range(TT):
                    last = v.scalar_tensor_tensor(h2[:, tt], x1[:, b, tt], mv2[:, tt, 0:1], mod[:, b, 4],
                                                  ALU.subtract, ALU.mult)
                link(last)

            def post_norm(b):
                dve.wait_ge(rstd2_ready, b + 1)
                for tt in range(TT):
                    last = v.scalar_tensor_tensor(h2[:, tt], h2[:, tt], rstd2[:, tt:tt + 1], mod[:, b, 3],
                                                  ALU.mult, ALU.add)
                last.then_inc(h2_ready, 1)

            def post_h2(b):
                r = full("h2T", b)
                if b >= 1:
                    dve.wait_ge(ring_full, USE[("logit", b - 1)] + 1)
                v.tensor_copy(h2T[:].rearrange("p t d -> p (t d)"), r[:]).then_inc(ring_free, 1)

            def post_logit(b):
                r = full("logit", b)
                v.tensor_tensor(lg[:, TT * b:TT * (b + 1)], r[:, 0:TT * E].rearrange("p (t e) -> p t e", e=E),
                                bsb[:].unsqueeze(1).to_broadcast([P, TT, E]), ALU.add).then_inc(ring_free, 1)
                dve.wait_ge(*freed("logit", b))

            def choose(b):
                n0, n1 = TT * b, TT * (b + 1)
                for n in range(n0, n1):
                    last = v.max(top[:, n], lg[:, n])
                link(last)
                for n in range(n0, n1):
                    last = v.max_index(topi[:, n], top[:, n], lg[:, n])
                link(last)
                link(v.tensor_copy(topf[:, n0:n1], topi[:, n0:n1]))
                for k in range(TOP):
                    last = v.tensor_tensor(oh[:, k, n0:n1], iota8[:].unsqueeze(1).to_broadcast([P, TT, E]),
                                           topf[:, n0:n1, k:k + 1].to_broadcast([P, TT, E]), ALU.is_equal)
                link(last)
                link(v.tensor_tensor(pick[:, n0:n1], oh[:, 0, n0:n1], oh[:, 1, n0:n1], ALU.add))
                for n in range(n0, n1):
                    link(v.tensor_tensor(before[:, n + 1], before[:, n], pick[:, n], ALU.add))

            def weights(n):
                dve.wait_ge(s_raw[n % 2], raw_count(n))
                if n < NW:
                    hi = (wgh, wuh)[n // E]
                    v.tensor_copy(hi[:, n % E], wraw[:, n % 2, 0:F]).then_inc(wsplit, 1)
                else:
                    v.tensor_copy(wdh[:, n - NW].rearrange("p k d -> p (k d)"), wraw[:, n % 2]).then_inc(wsplit, 1)

            def raw_count(n):
                return 16 * sum(1 if m < NW else 2 for m in range(n % 2, n + 1, 2))

            norms_center(0)
            norms_h(0)
            norms_hn(0)
            prep_xT(0)
            norms_center(1)
            norms_h(1)
            norms_hn(1)
            prep_rn(0)
            q = proj[:, :, 0:2 * D].rearrange("p t (g d) -> p t g d", d=HD)
            prep_dots(0)
            v.tensor_tensor(q, q, yr[:].rearrange("p (t g) -> p t g", t=TT).unsqueeze(3).to_broadcast(
                [P, TT, NG, HD]), ALU.mult).then_inc(qn_ready, 1)
            prep_gates(0)
            prep_lo(0)
            prep_operands(0, 0)
            for i in range(QUADS):
                value_operand(0, i)
            dve.wait_ge(consts_ready, 1)
            for b in range(B):
                more = b + 1 < B
                n = 3 * E // B * b
                if b >= 1:
                    fuse(b - 1)
                if more:
                    prep_xT(b + 1)
                if b >= 1:
                    value_operand(b, QUADS - 1)
                if more:
                    prep_qkv(b + 1, 0)
                weights(n)
                if b >= 1:
                    post_x1(b - 1)
                else:
                    prep_operands(0, 1)
                if more:
                    prep_qkv(b + 1, 1)
                if b >= 1:
                    post_center(b - 1)
                if more:
                    prep_qkv(b + 1, 2)
                if b >= 1:
                    post_norm(b - 1)
                if more:
                    prep_qkv(b + 1, 3)
                weights(n + 1)
                if b == 0:
                    prep_operands(0, 2)
                prep_gqt(b)
                if b == 0:
                    prep_operands(0, 3)
                if more:
                    prep_rn(b + 1)
                    prep_dots(b + 1)
                if b >= 1:
                    post_h2(b - 1)
                if b + 2 < B:
                    norms_center(b + 2)
                weights(n + 2)
                if more:
                    prep_gates(b + 1)
                if b >= 1:
                    post_logit(b - 1)
                if more:
                    prep_lo(b + 1)
                if b + 2 < B:
                    norms_h(b + 2)
                weights(n + 3)
                if b >= 1:
                    choose(b - 1)
                if b == 0:
                    mod_gates(0)
                    mod_gates(1)
                    dve.wait_ge(mod_ready, 2)
                if b + 2 < B:
                    norms_hn(b + 2)
                weights(n + 4)
                if more:
                    prep_operands(b + 1, 0)
                    for i in range(QUADS - 1):
                        value_operand(b + 1, i)
                weights(n + 5)
                if more:
                    for i in range(1, QUADS):
                        prep_operands(b + 1, i)
            fuse(B - 1)
            post_x1(B - 1)
            post_center(B - 1)
            post_norm(B - 1)
            post_h2(B - 1)
            post_logit(B - 1)
            choose(B - 1)
            dve.wait_ge(*freed("logit", B - 1))
            link(v.memset(hid[:, :, F:FC * P], 0.0))
            v.tensor_tensor(dl[:], top[:, :, 0], top[:, :, 1], ALU.subtract).then_inc(dl_ready, 1)
            dve.wait_ge(rank_ready, 1)
            rank, total = R[:, 0, 0:NT * E], R[:, 0, NT * E:NT * E + E]
            link(v.tensor_scalar(toti[:], total, float(P - 1), None, ALU.add))
            link(v.tensor_scalar(toti[:], toti[:], 7, None, ALU.arith_shift_right))
            link(v.tensor_copy(tot[:, 0], toti[:]))
            cur = 0
            for step in (1, 2, 4):
                v.tensor_copy(tot[:, cur + 1, 0:step], tot[:, cur, 0:step])
                link(v.tensor_tensor(tot[:, cur + 1, step:E], tot[:, cur, step:E], tot[:, cur, 0:E - step], ALU.add))
                cur += 1
            link(v.tensor_tensor(tbase[:], tot[:, 3], tot[:, 0], ALU.subtract))
            link(v.tensor_scalar(tbase[:], tbase[:], float(P), None, ALU.mult))
            link(v.tensor_tensor(slot3[:], rank.rearrange("p (n e) -> p n e", e=E),
                                 tbase[:].unsqueeze(1).to_broadcast([P, NT, E]), ALU.add))
            for k in range(TOP):
                last = v.tensor_tensor(slotm[:, k], oh[:, k], slot3[:], ALU.mult)
            link(last)
            link(v.tensor_reduce(slot[:], slotm[:].rearrange("p k n e -> p (k n) e"), AX_X, ALU.add))
            link(v.tensor_copy(sloti[:, 0], slot[:]))
            v.tensor_scalar(sloti[:, 1], sloti[:, 0], P - 1, None, ALU.bitwise_and)
            link(v.tensor_scalar(sloti[:, 2], sloti[:, 0], 7, None, ALU.arith_shift_right))
            link(v.tensor_copy(slotf[:], sloti[:, 1:3]))
            link(v.tensor_tensor(hi1h[:, :, 2], iotas[:].unsqueeze(1).to_broadcast([P, NK, SLOTS]),
                                 slotf[:, 1].unsqueeze(2).to_broadcast([P, NK, SLOTS]), ALU.is_equal))
            v.tensor_scalar(hi1h[:, :, 0], hi1h[:, :, 2], part1[:, 0:1], None, ALU.mult)
            v.tensor_tensor(hi1h[:, :, 1], hi1h[:, :, 2], knum[:, 0].unsqueeze(2).to_broadcast([P, NK, SLOTS]),
                            ALU.mult)
            v.tensor_tensor(hi1h[:, :, 2], hi1h[:, :, 2], knum[:, 1].unsqueeze(2).to_broadcast([P, NK, SLOTS]),
                            ALU.mult)
            for n in range(NK):
                v.tensor_scalar(lo1h[:, n], iotap[:], slotf[:, 0, n:n + 1], None,
                                ALU.is_equal).then_inc(onehot_ready, 1)
            link(v.tensor_tensor(eotc[:], iotas[:].unsqueeze(2).to_broadcast([P, SLOTS, E]),
                                 tot[:, 3].unsqueeze(1).to_broadcast([P, SLOTS, E]), ALU.is_ge))
            link(v.tensor_reduce(eotf[:], eotc[:], AX_X, ALU.add))
            v.tensor_scalar(eot[:], eotf[:], float(E - 1), None, ALU.min).then_inc(idx_ready, 1)
            dve.wait_ge(inv_ready, 1)
            got = R[:, 1, 0:3 * SLOTS].rearrange("p (a j) -> p a j", a=3)
            link(v.tensor_copy(inv[:, 0:3], got))
            link(v.tensor_scalar(inv[:, 3], inv[:, 1], float(P), -1.0, ALU.mult, ALU.add))
            link(v.tensor_tensor(inv[:, 1], inv[:, 3], inv[:, 0], ALU.add))
            v.tensor_scalar(gidx[:], inv[:, 1], 0.0, None, ALU.max)
            link(v.scalar_tensor_tensor(inv[:, 2], inv[:, 2], float(P), inv[:, 1], ALU.mult, ALU.add))
            link(v.tensor_scalar(inv[:, 0], inv[:, 0], 0.0, None, ALU.is_equal))
            link(v.tensor_tensor(inv[:, 0], inv[:, 0], spare[:], ALU.mult))
            v.tensor_tensor(sidx[:], inv[:, 0], inv[:, 2], ALU.add).then_inc(idx_ready, 1)
            dve.wait_ge(th_ready, 1)
            v.tensor_scalar(w12[:, 0], th[:], 0.5, 0.5, ALU.mult, ALU.add)
            link(v.tensor_scalar(w12[:, 1], th[:], -0.5, 0.5, ALU.mult, ALU.add))

            def turn_lo(m):
                k0, k1 = turn_parts(m)
                dve.wait_ge(turned_hi_ready, m + 4)
                v.tensor_tensor(turned_lo[:, m % 3, k0:k1], turn_bank(m),
                                turned_hi[:, m % 3, k0:k1].bitcast(F32), ALU.subtract).then_inc(turned_lo_ready, 1)

            turn_lo(-3)
            turn_lo(-2)
            for j in range(SLOTS + 2):
                if j < SLOTS:
                    dve.wait_ge(silu_ready, j + 1)
                    if j >= 2:
                        dve.wait_ge(turn_done, j + 2)
                    v.tensor_tensor(hid[:, j % 2, 0:F], sg[:, j % 2], S[:, j % 2, 1, 0:F],
                                    ALU.mult).then_inc(hid_ready, 1)
                if j <= SLOTS:
                    turn_lo(j - 1)
                if j >= 2:
                    m = j - 2
                    dve.wait_ge(down_done, m + 1)
                    if m >= GRING:
                        dve.wait_ge(scattered[m % GRING], 16 * (m // GRING))
                    v.tensor_copy(yv[:, m % GRING], R[:, m % 2, 0:D]).then_inc(y_ready, 1)

            for b in range(B):
                dve.wait_ge(y1_ready, b + 1)
                for tt in range(TT):
                    n = TT * b + tt
                    last = v.scalar_tensor_tensor(y12[0][:, n], y12[1][:, n], w12[:, 1, n:n + 1], y12[0][:, n],
                                                  ALU.mult, ALU.add)
                link(last)
                y = y12[0][:, TT * b:TT * (b + 1)]
                link(v.tensor_tensor(y, y, mod[:, b, 5].unsqueeze(1).to_broadcast([P, TT, D]), ALU.mult))
                v.tensor_tensor(x1[:, b], y, x1[:, b], ALU.add).then_inc(yo_ready, 1)

        @block.tensor
        def _(pe):
            mm = nc.tensor.matmul

            def claim(*key):
                n = USE[key]
                if n >= 3:
                    pe.wait_ge(*freed(*order[n - 3]))
                return R[:, n % 3]

            pe.wait_ge(silu_b_ready, 1)
            pe.wait_ge(s_wm, 16)
            def transposes(key, src):
                r = claim(*key)
                for tt in range(TT):
                    last = nc.tensor.transpose(r[:, tt * P:(tt + 1) * P], src(tt), ident[:])
                last.then_inc(ring_full, 1)

            def prep_x(b):
                pe.wait_ge(hn_ready, b + 1)
                transposes(("h", b), lambda tt: hh[:, tt])
                transposes(("hn", b), lambda tt: hn[:, tt])

            def prep_qkv(b, tt):
                r = claim("qkv", b, tt)
                pe.wait_ge(*freed("hn", b))
                mm(r[:, 0:2 * D + NG], xnT[:, tt], wproj[:, 0:2 * D + NG], start=True, stop=True)
                mm(r[:, 2 * D + NG:PROJ], hT[:, tt], wvp, start=True, stop=True).then_inc(ring_full, 1)

            def prep_gate(b):
                pe.wait_ge(gqe_ready, b + 1)
                transposes(("gate", b), lambda tt: gqe[:, tt])
                r = claim("csum", b)
                for tt in range(TT):
                    last = mm(r[:, 0:1], gv[:, tt], ones[:], start=tt == 0, stop=tt == TT - 1)
                last.then_inc(ring_full, 1)

            def turn_qk(b):
                pe.wait_ge(qn_ready, b + 1)
                transposes(("qT", b), lambda tt: proj[:, tt, 0:D])
                transposes(("kT", b), lambda tt: proj[:, tt, D:2 * D])

            def prep_operand(b, i):
                rows = slice(32 * i, 32 * i + 32)
                pe.wait_ge(*freed("kT", b))
                for name, a in (("q", 0), ("k", 1)):
                    r = claim(name, b, i)
                    mm(r[:], spread[rows, 2 * a], qkT_hi[rows, a], start=True, stop=False)
                    mm(r[:], spread[rows, 2 * a + 1], qkT_lo[rows, a], start=False, stop=True
                       ).then_inc(ring_full, 1)

            def scores(b, s):
                i, kt = s // TT, s % TT
                if kt == 0:
                    pe.wait_ge(*freed("q", b, i))
                    pe.wait_ge(*freed("k", b, i))
                for pr in range(2):
                    n = 2 * (STEPS * b + s) + pr
                    if n >= 2:
                        pe.wait_ge(tanh_ready, n - 1)
                    if pr == 0 and (s in HEAT_STEPS or b == B - 1 or (b == 0 and s in (6, 7))):
                        heat(S[:, 0, 0], 1)
                    for u in range(2):
                        r0 = 32 * (2 * pr + u)
                        last = mm(S[:, pr, u], KA[r0:r0 + 32, i, kt * P:(kt + 1) * P], QA[r0:r0 + 32, i, :],
                                  start=True, stop=True)
                    last.then_inc(scores_ready, 1)

            def values(b, s):
                i, kt = s // TT, s % TT
                if s == 0 and b >= 1:
                    pe.wait_ge(fused_ready, b)
                if kt == 0:
                    pe.wait_ge(gvz_ready, QUADS * b + i + 1)
                for lane in range(LANES):
                    n = 2 * (STEPS * b + s) + lane // 2
                    pe.wait_ge(tanh_ready, n + 1)
                    last = mm(AV[32 * lane:32 * lane + 32, :], gvz[:, kt, i, lane], tanh[:, n % 4, lane % 2],
                              start=s == 0, stop=s == STEPS - 1)
                last.then_inc(av_done, 1)

            def post(b, part):
                if part == 0:
                    pe.wait_ge(fused_ready, b + 1)
                    r = claim("wo", b)
                    for tt in range(TT):
                        last = mm(r[:, tt * P:(tt + 1) * P], fT[:, tt * P:(tt + 1) * P], wo[:], start=True, stop=True)
                    last.then_inc(ring_full, 1)
                elif part == 1:
                    pe.wait_ge(h2_ready, b + 1)
                    transposes(("h2T", b), lambda tt: h2[:, tt])
                else:
                    r = claim("logit", b)
                    pe.wait_ge(*freed("h2T", b))
                    for tt in range(TT):
                        last = mm(r[:, tt * E:(tt + 1) * E], h2T[:, tt], ws[:], start=True, stop=True)
                    last.then_inc(ring_full, 1)

            def heat(to, count):
                for _ in range(count):
                    mm(to, warm[:, 0:P], warm[:], start=True, stop=True)

            for n in range(2 * B):
                b, half = n // 2, n % 2
                r = claim("mod", b, half)
                mm(r[:, 0:3 * D], silub[:, b], wm[:, 3 * half * D:3 * (half + 1) * D], start=True,
                   stop=True).then_inc(ring_full, 1)
                if n == MODS_FIRST - 1:
                    pe.wait_ge(ident_ready, 1)
                    prep_x(0)
            pe.wait_ge(wvp_ready, 1)
            pe.wait_ge(wgate_ready, 1)
            for tt in range(TT):
                prep_qkv(0, tt)
            pe.wait_ge(consts_ready, 1)
            heat(AV[:], HEAT_FIRST)
            turn_qk(0)
            heat(AV[:], 6)
            prep_operand(0, 0)
            for b in range(B):
                more = b + 1 < B
                for s in range(STEPS):
                    scores(b, s)
                    if s > 0:
                        values(b, s - 1)
                    elif b > 0:
                        values(b - 1, STEPS - 1)
                    if s == 0 and more:
                        prep_x(b + 1)
                    if s == 2 and b >= 1:
                        pe.wait_ge(s_wo, 16 * HEADS)
                        post(b - 1, 0)
                    if s in (1, 2, 3, 4) and more:
                        prep_qkv(b + 1, s - 1)
                    if b == 0 and s in FIRST_STEPS[:2]:
                        prep_operand(0, 1 + FIRST_STEPS.index(s))
                    if s == 5:
                        prep_gate(b)
                    if b == 0 and s == FIRST_STEPS[2]:
                        prep_operand(0, 3)
                    if s in POST_STEPS and b >= 1:
                        post(b - 1, 1 + POST_STEPS.index(s))
                    if more and s == TURN_STEP:
                        turn_qk(b + 1)
                    if more and s in OPERAND_STEPS:
                        prep_operand(b + 1, OPERAND_STEPS.index(s))
            values(B - 1, STEPS - 1)
            for part in range(3):
                post(B - 1, part)

            pe.wait_ge(dl_ready, 1)
            rank = R[:, 0, 0:NT * E]
            mm(rank, onesq[:], before[:, 0:NT].rearrange("p n e -> p (n e)"), start=True, stop=False)
            mm(rank, tri[:], pick[:].rearrange("p n e -> p (n e)"), start=False, stop=True)
            mm(R[:, 0, NT * E:NT * E + E], onesq[:], before[:, NT], start=True, stop=True).then_inc(rank_ready, 1)
            for n in range(NK):
                pe.wait_ge(onehot_ready, n + 1)
                last = mm(R[:, 1, 0:3 * SLOTS], lo1h[:, n], hi1h[:, n].rearrange("p a j -> p (a j)"),
                          start=n == 0, stop=n == NK - 1)
            last.then_inc(inv_ready, 1)

            pe.wait_ge(wlo, 3 * E)
            pe.wait_ge(idx_ready, 2)

            def expert(j):
                return nc.tensor.value_load(eot[0:1, j:j + 1], min_val=0, max_val=E - 1)

            def up(j, e):
                pe.wait_ge(turned_lo_ready, j + 1)
                if j >= 2:
                    pe.wait_ge(hid_ready, j - 1)
                G, U = S[:, j % 2, 0, 0:F], S[:, j % 2, 1, 0:F]
                hi, lo = turned_hi[:, j % 3, FC], turned_lo[:, j % 3, FC]

                def w(t):
                    return t[:, bass.ds(e, 1)].rearrange("p a f -> p (a f)")

                mm(G, hi, w(wgh), start=True, stop=False)
                mm(G, hi, w(wgl), start=False, stop=False)
                mm(U, hi, w(wuh), start=True, stop=False)
                mm(U, hi, w(wul), start=False, stop=False)
                mm(G, lo, w(wgh), start=False, stop=True)
                mm(U, lo, w(wuh), start=False, stop=True).then_inc(gu_ready, 1)

            def turn(m):
                if m >= -1:
                    pe.wait_ge(turned_lo_ready, m + 2)
                if m >= 0:
                    pe.wait_ge(hid_ready, m + 1)
                if m + 3 < SLOTS:
                    pe.wait_ge(gathered[(m + 3) % GRING], 16 * ((m + 3) // GRING + 1))
                k0, k1 = turn_parts(m)
                for k in range(k0, k1):
                    src = hid[:, m % 2, k * P:(k + 1) * P] if k < FC else xg[:, (m + 3) % GRING]
                    last = nc.tensor.transpose(turn_bank(m)[:, k - k0], src, ident[:])
                last.then_inc(turn_done, 1)

            def down(j, e):
                pe.wait_ge(turned_lo_ready, j + 4)
                if j >= 2:
                    pe.wait_ge(y_ready, j - 1)
                y = R[:, j % 2, 0:D]

                def w(t, k, rows):
                    return t[0:rows, bass.ds(e, 1), k].rearrange("p a d -> p (a d)")

                for k in range(FC):
                    rows = P if k < FC - 1 else FLAST
                    hi, lo = turned_hi[0:rows, j % 3, k], turned_lo[0:rows, j % 3, k]
                    mm(y, hi, w(wdh, k, rows), start=k == 0, stop=False)
                    mm(y, hi, w(wdl, k, rows), start=False, stop=False)
                    last = mm(y, lo, w(wdh, k, rows), start=False, stop=k == FC - 1)
                last.then_inc(down_done, 1)

            es = {}
            turn(-3)
            turn(-2)
            for j in range(SLOTS + 2):
                if j < SLOTS:
                    es[j] = expert(j)
                    up(j, es[j])
                if j <= SLOTS:
                    turn(j - 1)
                if j >= 2:
                    down(j - 2, es[j - 2])


_INS = ["x", "w_q", "w_k", "w_v", "g_q", "g_k", "w_o", "b_o", "gamma", "beta"]
_FFN = ["Ws", "bs", "Wg", "Wu", "Wd"]


def kernel(**inputs):
    import numpy as np
    import concourse.bacc as bacc
    from concourse.bass_utils import run_bass_kernel_spmd

    nc = bacc.Bacc("TRN2", target_bir_lowering=False, num_devices=1)
    names = ["L0_attn_" + n for n in _INS] + ["L0_ffn_" + n for n in _FFN] + ["L0_c", "L0_wmod"]
    arrays, args = {}, []
    for name in names:
        a = np.ascontiguousarray(inputs[name])
        arrays[f"in_{name}"] = a
        args.append(nc.dram_tensor(f"in_{name}", a.shape, mybir.dt.from_np(a.dtype), kind="ExternalInput").ap())
    out = nc.dram_tensor("out_x", arrays["in_L0_attn_x"].shape, F32, kind="ExternalOutput").ap()
    adaln_block(nc, *args, out)
    r = run_bass_kernel_spmd(nc, [arrays], core_ids=[0])
    return r.results[0]["out_x"]
```

```python
from contextlib import ExitStack

import concourse.bass as bass
from concourse import mybir

ALU = mybir.AluOpType
ACT = mybir.ActivationFunctionType
AX_X = mybir.AxisListType.X
F32 = mybir.dt.float32
F32R = mybir.dt.float32r
I32 = mybir.dt.int32
U32 = mybir.dt.uint32
BF16 = mybir.dt.bfloat16

P = 128
HEADS = 16
QUADS = 4
LANES = 4
THRESHOLD = 0.27
SHARPNESS = 15.0
LN_EPS = 1e-5
NORM_EPS = 1e-12
RSQRT_MAGIC = 0x5F3759DF


def adaln_block(nc, x, w_q, w_k, w_v, g_q, g_k, w_o, b_o, gamma, beta, Ws, bs, Wg, Wu, Wd, c, wmod, out):
    B, T, D = x.shape
    HD = D // HEADS
    TT = T // P
    E, _, F = Wg.shape
    FC = -(-F // P)
    FLAST = F - (FC - 1) * P
    NT = B * TT
    TOP = 2
    NK = TOP * NT
    SLOTS = NK + E - 1
    XRING = 10
    YRING = 4
    AHEAD = XRING - 1
    STEPS = QUADS * TT
    POST_STEPS = (6, 8)
    GATE_STEP, TURN_STEP, OPERAND_STEPS = 8, 9, (12, 13, 14, 15)
    FIRST_STEPS = (1, 4, 5)
    HEAT_STEPS = (5, 6, 7, 8, 9, 10, 11, 12, 14)
    HEAT_SUMS = 2
    HEAT_START = (6, 20, 8, 4)
    HEAT_COUNTS = (20, 4, 10, 24, 10)
    ROWS_POOL = 10
    MODS_FIRST = 4
    NG = 2 * HEADS
    PROJ = 3 * D + NG
    assert D == P and HD == 8 and T == TT * P and LANES * QUADS == HEADS and TT == 4

    ctx = ExitStack()
    with ctx:
        def sb(name, shape, dt=F32):
            return ctx.enter_context(nc.sbuf_tensor(name, shape, dt))

        def sem(name):
            return ctx.enter_context(nc.semaphore(name))

        tanh = sb("tanh", [P, 4, 2, T])
        wm = tanh[:, 0].rearrange("p a t -> p (a t)")[:, 0:6 * D]
        silub = tanh[:, 1].rearrange("p a t -> p (a t)")[:, 0:B * P].rearrange("p (b q) -> p b q", b=B)
        sg = tanh[:, 2, :, 0:F]
        hid = tanh[:, 3, :, 0:FC * P]
        ident = sb("ident", [P, P])
        ones = sb("ones", [P, 1])
        mhalf = sb("mhalf", [P, TT])
        warm = sb("warm", [P, 512], BF16)
        tanh_bias = sb("tanh_bias", [P, 1])
        wproj = sb("wproj", [P, PROJ])
        wqk = wproj[:, 0:2 * D]
        wgate = wproj[:, 2 * D:2 * D + NG]
        wvp = wproj[:, 2 * D + NG:PROJ]
        wv = sb("wv", [P, D])
        head32 = sb("head32", [P, 32])
        spread = sb("spread", [P, 4, P], F32R)
        wo = sb("wo", [P, D])
        wog = sb("wog", [P, B, D])
        ws = sb("ws", [P, E])
        bsb = sb("bsb", [P, E])
        gqk = sb("gqk", [P, 2, HD])
        gam = sb("gam", [P, 1])
        bet = sb("bet", [P, 1])
        bo = sb("bo", [P, D])
        cT = sb("cT", [P, B])
        siluc = sb("siluc", [P, B])
        mod = sb("mod", [P, B, 6, D])
        gab = sb("gab", [P, B, D])
        wgh = sb("wgh", [P, E, F], F32R)
        wgl = sb("wgl", [P, E, F], F32R)
        wuh = sb("wuh", [P, E, F], F32R)
        wul = sb("wul", [P, E, F], F32R)
        wd = sb("wd", [P, E, FC, 2, D], F32R)
        wraw = sb("wraw", [P, 2, FC * D])
        iota8 = sb("iota8", [P, E])
        xin = sb("xin", [P, B, TT, D])
        x1 = xin
        h2T = sb("h2T", [P, TT, D])
        lg = sb("lg", [P, NT, E])
        h2rows = nc.dram_tensor("h2rows", (NT * P, D), F32, kind="Internal").ap()
        yrows = nc.dram_tensor("yrows", ((NK + SLOTS) * P, D), F32, kind="Internal").ap()
        st = sb("st", [P, TT, 6])
        mv = sb("mv", [P, TT, 2])
        ve = sb("ve", [P, TT])
        rstd = sb("rstd", [P, TT])
        room = sb("room", [P, 4, TT * D])
        hh, hn, hT, xnT = (room[:, n].rearrange("p (t d) -> p t d", t=TT) for n in range(4))
        qkT_hi = sb("qkT_hi", [P, 2, TT * P], F32R)
        qkT_lo = sb("qkT_lo", [P, 2, TT * P], F32R)
        spread_f = room[:, 3].rearrange("p (k q) -> p k q", q=P)
        proj = sb("proj", [P, TT, PROJ])
        sq = sb("sq", [P, TT, 2 * D])
        ss = sb("ss", [P, TT * NG])
        yr = sb("yr", [P, TT * NG])
        yt = sb("yt", [P, TT * NG])
        dots = sb("dots", [P, TT, NG])
        gt = sb("gt", [P, TT, NG])
        gate = sb("gate", [P, TT, NG])
        gqe = sb("gqe", [P, TT, D])
        gv = sb("gv", [P, TT, D])
        gvsum = sb("gvsum", [P, D])
        gvz = sb("gvz", [P, TT, QUADS, LANES, 32])
        QA = sb("QA", [P, QUADS, TT * P], F32R)
        KA = sb("KA", [P, QUADS, TT * P], F32R)
        GQT = sb("GQT", [P, TT * P])
        Cs = sb("Cs", [P, 1])
        fT = sb("fT", [P, TT * P])
        xb = sb("xb", [P, TT, D])
        st2 = sb("st2", [P, TT, 6])
        mv2 = sb("mv2", [P, TT, 2])
        ve2 = sb("ve2", [P, TT])
        rstd2 = sb("rstd2", [P, TT])
        h2 = sb("h2", [P, TT, D])
        tri = sb("tri", [P, P], BF16)
        onesq = sb("onesq", [P, P], BF16)
        iotap = sb("iotap", [P, P], BF16)
        iotas = sb("iotas", [P, SLOTS], BF16)
        part1 = sb("part1", [P, 1])
        picks = sb("picks", [P, NK], BF16)
        spare = sb("spare", [P, SLOTS])
        top = sb("top", [P, NT, 8])
        topi = sb("topi", [P, NT, 8], U32)
        topf = sb("topf", [P, NT, 8])
        dl = sb("dl", [P, NT])
        th = sb("th", [P, NT])
        w12 = sb("w12", [P, TOP, NT])
        oh = sb("oh", [P, TOP, NT, E])
        pick = sb("pick", [P, NT, E], BF16)
        before = sb("before", [P, NT + 1, E], BF16)
        tot = sb("tot", [P, 4, E])
        toti = sb("toti", [P, E], I32)
        tend = sb("tend", [P, E])
        tbase = sb("tbase", [P, E])
        slot3 = sb("slot3", [P, NT, E])
        slotm = sb("slotm", [P, TOP, NT, E])
        slot = sb("slot", [P, NK])
        sloti = sb("sloti", [P, 3, NK], I32)
        slot_row = sb("slot_row", [P, NK])
        slot_tile = sb("slot_tile", [P, NK], BF16)
        lo1h = gvz[:].rearrange("p t i j e -> p (t i j e)").bitcast(BF16)[:, 0:NK * P].rearrange(
            "p (n q) -> p n q", q=P)
        hi1h = room[:].rearrange("p a q -> p (a q)").bitcast(BF16)[:, 0:NK * 3 * SLOTS].rearrange(
            "p (n a j) -> p n a j", n=NK, a=3)
        eotc = sb("eotc", [P, SLOTS, E])
        eotf = sb("eotf", [P, SLOTS])
        eot = sb("eot", [P, SLOTS], I32)
        inv = sb("inv", [P, 3, SLOTS])
        gnum = sb("gnum", [P, SLOTS], I32)
        gidx = sb("gidx", [P, SLOTS], I32)
        sidx = sb("sidx", [P, SLOTS], I32)
        xg = sb("xg", [P, XRING, D])
        yv = sb("yv", [P, YRING, D])
        turned_hi = QA[:, 0:3].rearrange("p a (k q) -> p a k q", k=FC + 1)
        turned_lo = KA[:, 0:3].rearrange("p a (k q) -> p a k q", k=FC + 1)
        y12 = (room[:].rearrange("p a (t d) -> p (a t) d", d=D),
               gvz[:].rearrange("p t i j e -> p (t i j e)").rearrange("p (n d) -> p n d", d=D))

        S = ctx.enter_context(nc.psum_tensor("S", [P, 2, 2, 512], F32))
        AV = ctx.enter_context(nc.psum_tensor("AV", [P, 512], F32))
        R = ctx.enter_context(nc.psum_tensor("R", [P, 3, 512], F32))

        s_gates = sem("s_gates")
        s_c, s_wm, s_wqkv, s_small, s_bo = sem("s_c"), sem("s_wm"), sem("s_wqkv"), sem("s_small"), sem("s_bo")
        s_x = [sem(f"s_x{b}") for b in range(B)]
        s_wo = sem("s_wo")
        s_raw = [sem("s_raw0"), sem("s_raw1")]
        out_stored = sem("out_stored")
        ident_ready = sem("ident_ready")
        consts_ready = sem("consts_ready")
        warm_ready = sem("warm_ready")
        silu_c_ready = sem("silu_c_ready")
        silu_b_ready = sem("silu_b_ready")
        mod_copied = sem("mod_copied")
        mod_ready = sem("mod_ready")
        spread_ready = sem("spread_ready")
        wgate_ready = sem("wgate_ready")
        wog_ready = sem("wog_ready")
        wvp_ready = sem("wvp_ready")
        gab_ready = sem("gab_ready")
        dve_chain = sem("dve_chain")
        pool_chain = sem("pool_chain")
        var_ready = sem("var_ready")
        rstd_ready = sem("rstd_ready")
        h_ready = sem("h_ready")
        hn_ready = sem("hn_ready")
        xT_ready = sem("xT_ready")
        qkv_ready = sem("qkv_ready")
        sq_ready = sem("sq_ready")
        rn_ready = sem("rn_ready")
        qn_ready = sem("qn_ready")
        hi_ready = sem("hi_ready")
        lo_ready = sem("lo_ready")
        dots_ready = sem("dots_ready")
        gt_ready = sem("gt_ready")
        gate_ready = sem("gate_ready")
        gv_ready = sem("gv_ready")
        gqe_ready = sem("gqe_ready")
        gvz_ready = sem("gvz_ready")
        gvsum_ready = sem("gvsum_ready")
        ring_full = sem("ring_full")
        ring_free = sem("ring_free")
        ring_free_act = sem("ring_free_act")
        scores_ready = sem("scores_ready")
        tanh_ready = sem("tanh_ready")
        av_done = sem("av_done")
        fused_ready = sem("fused_ready")
        xb_ready = sem("xb_ready")
        var2_ready = sem("var2_ready")
        rstd2_ready = sem("rstd2_ready")
        h2_ready = sem("h2_ready")
        h2_stored = sem("h2_stored")
        route_in = sem("route_in")
        counts_ready = sem("counts_ready")
        rank_ready = sem("rank_ready")
        slot_ready = sem("slot_ready")
        onehot_ready = sem("onehot_ready")
        onehot_pool_ready = sem("onehot_pool_ready")
        tile_onehot_ready = sem("tile_onehot_ready")
        payload_ready = sem("payload_ready")
        inv_ready = sem("inv_ready")
        idx_ready = sem("idx_ready")
        gathered = [sem(f"gathered{i}") for i in range(XRING)]
        scattered = [sem(f"scattered{i}") for i in range(YRING)]
        turn_done = sem("turn_done")
        turned_hi_ready = sem("turned_hi_ready")
        turned_lo_ready = sem("turned_lo_ready")
        y_loaded = [sem(f"y_loaded{b}") for b in range(B)]
        y1_ready = sem("y1_ready")
        mix_ready = sem("mix_ready")
        split_ready = sem("split_ready")
        wsplit = sem("wsplit")
        wlo = sem("wlo")
        dl_ready = sem("dl_ready")
        th_ready = sem("th_ready")
        gu_ready = sem("gu_ready")
        silu_ready = sem("silu_ready")
        hid_ready = sem("hid_ready")
        down_done = sem("down_done")
        y_ready = sem("y_ready")
        y2_ready = sem("y2_ready")
        yg_ready = sem("yg_ready")
        yo_ready = [sem(f"yo_ready{b}") for b in range(B)]

        TURNS = range(-3, SLOTS)

        def turn_parts(m):
            return 0 if m >= 0 else FC, FC + 1 if m + 3 < SLOTS else FC

        def turn_bank(m):
            k0, k1 = turn_parts(m)
            return (AV[:], R[:, 2])[m % 2][:, k0 * P:k1 * P].rearrange("p (k q) -> p k q", q=P)

        assert F <= FC * P and (FC + 1) * P == 512

        xs = x.rearrange("b (p t) d -> p b t d", t=TT)
        outs = out.rearrange("b (p t) d -> p b t d", t=TT)
        NW = 2 * E

        block = ctx.enter_context(nc.Block())

        USE = {}
        order = []

        def use(*key):
            USE[key] = len(order)
            order.append(key)

        def by_scalar(key):
            return key[0] == "q" or key[0:2] == ("qkv", 0) or (key[0] == "mod" and key[1:] != (0, 0))

        def freed(*key):
            mine = by_scalar(key)
            count = sum(1 for k in order[:USE[key] + 1] if by_scalar(k) == mine)
            return (ring_free_act if mine else ring_free), count

        def operand_uses(b, i):
            use("q", b, i)
            use("k", b, i)

        for n in range(2 * B):
            use("mod", n // 2, n % 2)
            if n == MODS_FIRST - 1:
                use("h", 0)
                use("hn", 0)
                for tt in range(TT):
                    use("qkv", 0, tt)
        use("qT", 0)
        use("kT", 0)
        operand_uses(0, 0)
        for b in range(B):
            more = b + 1 < B
            if more:
                use("h", b + 1)
                use("hn", b + 1)
                use("qkv", b + 1, 0)
            if b == 0:
                operand_uses(0, 1)
            if b >= 1:
                use("wo", b - 1)
            if more:
                for tt in range(1, TT):
                    use("qkv", b + 1, tt)
            if b == 0:
                operand_uses(0, 2)
            use("gate", b)
            use("csum", b)
            if b == 0:
                operand_uses(0, 3)
            if b >= 1:
                use("h2T", b - 1)
                use("logit", b - 1)
            if more:
                use("qT", b + 1)
                use("kT", b + 1)
                for i in range(QUADS):
                    operand_uses(b + 1, i)
        use("wo", B - 1)
        use("h2T", B - 1)
        use("logit", B - 1)

        @block.sync
        def _(sp):
            sp.dma_start(wm[:], wmod).then_inc(s_wm, 16)
            sp.dma_start(xin[:, 0], xs[:, 0]).then_inc(s_x[0], 16)
            sp.dma_start(wqk[:, 0:D], w_q).then_inc(s_wqkv, 16)
            sp.dma_start(wqk[:, D:2 * D], w_k).then_inc(s_wqkv, 16)
            sp.dma_start(wv[:], w_v).then_inc(s_wqkv, 16)
            for lane in range(LANES):
                src = w_o.rearrange("(i j d) n -> j i d n", i=QUADS, j=LANES)[lane]
                for i in range(QUADS):
                    r0 = 32 * lane + HD * i
                    sp.dma_start(wo[r0:r0 + HD, :], src[i]).then_inc(s_wo, 16)
            for b in range(1, B):
                sp.dma_start(xin[:, b], xs[:, b]).then_inc(s_x[b], 16)
            sp.dma_start(bo[:], b_o.partition_broadcast(P)).then_inc(s_bo, 16)
            sp.wait_ge(consts_ready, 1)
            for n in range(3 * E):
                if n >= 2:
                    sp.wait_ge(wlo, n - 1)
                if n < NW:
                    W = Wg if n < E else Wu
                    sp.dma_start(wraw[:, n % 2, 0:F], W[n % E]).then_inc(s_raw[n % 2], 16)
                else:
                    e = n - NW
                    sp.dma_start(wraw[:, n % 2, 0:(FC - 1) * D],
                                 Wd[e, 0:(FC - 1) * P].rearrange("(k p) d -> p k d", p=P)).then_inc(s_raw[n % 2], 16)
                    sp.dma_start(wraw[0:FLAST, n % 2, (FC - 1) * D:FC * D],
                                 Wd[e, (FC - 1) * P:F]).then_inc(s_raw[n % 2], 16)
            yr_v = yrows[0:NK * P].rearrange("(k b t p) d -> b k p t d", k=TOP, b=B, t=TT)
            for i in range(YRING):
                sp.wait_ge(scattered[i], 16 * len(range(i, SLOTS, YRING)))
            for b in range(B):
                for k in range(TOP):
                    sp.dma_start(y12[k][:, TT * b:TT * (b + 1)], yr_v[b, k]).then_inc(y_loaded[b], 16)
            for b in range(B):
                sp.wait_ge(yo_ready[b], 1)
                sp.dma_start(outs[:, b], x1[:, b]).then_inc(out_stored, 16)
            sp.wait_ge(out_stored, 16 * B)

        @block.gpsimd
        def _(pool):
            g = nc.gpsimd
            chain = [0]

            def link(ins):
                chain[0] += 1
                ins.then_inc(pool_chain, 1)
                pool.wait_ge(pool_chain, chain[0])

            link(g.memset(ident[:], 0.0))
            g.affine_select(out=ident[:], in_=ident[:], compare_op=ALU.not_equal, fill=1.0, base=0,
                            pattern=[[-1, P]], channel_multiplier=1).then_inc(ident_ready, 1)
            g.memset(mhalf[:], -0.5)
            g.memset(warm[:], 1.0).then_inc(warm_ready, 1)
            g.memset(gvz[:], 0.0)
            g.memset(wraw[:], 0.0)
            g.memset(tanh_bias[:], -THRESHOLD * SHARPNESS)
            g.memset(ones[:], 1.0)
            g.memset(onesq[:], 1.0)
            g.memset(before[:, 0], 0.0)
            link(g.memset(tri[:], 1.0))
            g.affine_select(out=tri[:], in_=tri[:], compare_op=ALU.is_gt, fill=0.0, base=0,
                            pattern=[[1, P]], channel_multiplier=-1)
            g.iota(iotap[:], [[1, P]], base=0, channel_multiplier=0, allow_small_or_imprecise_dtypes=True)
            g.iota(iotas[:], [[1, SLOTS]], base=0, channel_multiplier=0, allow_small_or_imprecise_dtypes=True)
            g.iota(part1[:], [[0, 1]], base=1, channel_multiplier=1, allow_small_or_imprecise_dtypes=True)
            g.iota(spare[:], [[P, SLOTS]], base=NK * P + 1, channel_multiplier=1,
                   allow_small_or_imprecise_dtypes=True)
            g.iota(picks[:], [[1, NK]], base=0, channel_multiplier=0, allow_small_or_imprecise_dtypes=True)
            g.iota(iota8[:], [[1, E]], base=0, channel_multiplier=0,
                   allow_small_or_imprecise_dtypes=True).then_inc(consts_ready, 1)
            pool.wait_ge(s_wqkv, 48)
            g.tensor_copy(wvp.rearrange("p (j i d) -> p i j d", j=LANES, i=QUADS),
                          wv[:].rearrange("p (i j d) -> p i j d", i=QUADS, j=LANES)).then_inc(wvp_ready, 1)

            def power(dst, src, ready, n):
                pool.wait_ge(ready, n)
                return g.tensor_tensor(dst, src, mhalf[:], ALU.pow)

            def weights(n):
                pool.wait_ge(wsplit, n + 1)
                if n < NW:
                    hi, lo = ((wgh, wgl), (wuh, wul))[n // E]
                    e = n % E
                    g.tensor_tensor(lo[:, e], wraw[:, n % 2, 0:F], hi[:, e].bitcast(F32),
                                    ALU.subtract).then_inc(wlo, 1)
                else:
                    e = n - NW
                    g.tensor_tensor(wd[:, e, :, 1], wraw[:, n % 2].rearrange("p (k d) -> p k d", d=D),
                                    wd[:, e, :, 0].bitcast(F32), ALU.subtract).then_inc(wlo, 1)

            def norm(b, which):
                power(rstd[:], ve[:], var_ready, 2 * b + which + 1).then_inc(rstd_ready, 1)

            def squares(b, half):
                t0, t1 = half * TT // 2, (half + 1) * TT // 2
                pool.wait_ge(*freed("qkv", b, t1 - 1))
                if b >= 1:
                    pool.wait_ge(rn_ready, b)
                g.tensor_tensor(sq[:, t0:t1], proj[:, t0:t1, 0:2 * D], proj[:, t0:t1, 0:2 * D],
                                ALU.mult).then_inc(sq_ready, 1)

            def unit_qk(b):
                pool.wait_ge(rn_ready, b + 1)
                q = proj[:, :, 0:2 * D].rearrange("p t (g d) -> p t g d", d=HD)
                g.tensor_tensor(q, q, yr[:].rearrange("p (t g) -> p t g", t=TT).unsqueeze(3).to_broadcast(
                    [P, TT, NG, HD]), ALU.mult).then_inc(qn_ready, 1)

            def gated(b):
                pool.wait_ge(gate_ready, b + 1)
                if b >= 1:
                    pool.wait_ge(ring_full, USE[("csum", b - 1)] + 1)
                    pool.wait_ge(gvz_ready, QUADS * b)
                    pool.wait_ge(gvsum_ready, b)
                for tt in range(TT):
                    gk = gate[:, tt, HEADS:NG].rearrange("p (i j) -> p j i", j=LANES)
                    last = g.tensor_tensor(gv[:, tt].rearrange("p (j i d) -> p j i d", j=LANES, d=HD),
                                           proj[:, tt, 2 * D + NG:PROJ].rearrange(
                                               "p (j i d) -> p j i d", j=LANES, d=HD),
                                           gk.unsqueeze(3).to_broadcast([P, LANES, QUADS, HD]), ALU.mult)
                last.then_inc(gv_ready, 1)
                for tt in range(TT):
                    gq = gate[:, tt, 0:HEADS].rearrange("p (i j) -> p j i", j=LANES)
                    last = g.tensor_copy(gqe[:, tt].rearrange("p (j i d) -> p j i d", j=LANES, d=HD),
                                         gq.unsqueeze(3).to_broadcast([P, LANES, QUADS, HD]))
                last.then_inc(gqe_ready, 1)

            def residual(b):
                if b >= 1:
                    pool.wait_ge(var2_ready, b)
                g.tensor_tensor(xb[:], xin[:, b], gab[:, b].unsqueeze(1).to_broadcast([P, TT, D]),
                                ALU.add).then_inc(xb_ready, 1)

            def store_h2(b):
                pool.wait_ge(h2_ready, b + 1)
                pool.dma_start(h2rows[TT * P * b:TT * P * (b + 1)].rearrange("(t p) d -> p t d", p=P),
                               h2[:]).then_inc(h2_stored, 16)

            def norm2(b):
                power(rstd2[:], ve2[:], var2_ready, b + 1).then_inc(rstd2_ready, 1)

            norm(0, 0)
            norm(0, 1)
            norm(1, 0)
            norm(1, 1)
            gated(0)
            for b in range(B):
                more = b + 1 < B
                n = 3 * E // B * b
                if b >= 1:
                    residual(b - 1)
                weights(n)
                if b >= 1:
                    norm2(b - 1)
                if more:
                    squares(b + 1, 0)
                    squares(b + 1, 1)
                if b >= 1:
                    store_h2(b - 1)
                weights(n + 1)
                if more:
                    unit_qk(b + 1)
                if b + 2 < B:
                    norm(b + 2, 0)
                weights(n + 2)
                if more:
                    gated(b + 1)
                if b + 2 < B:
                    norm(b + 2, 1)
                weights(n + 3)
                if b == 0:
                    pool.wait_ge(mod_ready, 2)
                    pool.wait_ge(s_bo, 16)
                    g.tensor_tensor(gab[:], mod[:, :, 2], bo[:].unsqueeze(1).to_broadcast([P, B, D]),
                                    ALU.mult).then_inc(gab_ready, 1)
                    pool.wait_ge(gab_ready, 1)
                weights(n + 4)
                weights(n + 5)
            residual(B - 1)
            norm2(B - 1)
            store_h2(B - 1)

            pool.wait_ge(slot_ready, 1)
            for n in range(ROWS_POOL):
                g.tensor_scalar(lo1h[:, n], iotap[:], slot_row[:, n:n + 1], None,
                                ALU.is_equal).then_inc(onehot_pool_ready, 1)
            pool.wait_ge(h2_stored, 16 * B)
            pool.wait_ge(idx_ready, 2)

            def gather(j):
                if j >= XRING:
                    pool.wait_ge(turn_done, j - XRING + 1)
                pool.indirect_dma_start(xg[:, j % XRING], None, h2rows,
                                        bass.IndirectOffsetOnAxis(ap=gidx[:, j:j + 1], axis=0)
                                        ).then_inc(gathered[j % XRING], 16)

            for j in range(AHEAD):
                gather(j)
            for j in range(SLOTS):
                if j + AHEAD < SLOTS:
                    gather(j + AHEAD)
                if j == 0:
                    pool.wait_ge(idx_ready, 3)
                pool.wait_ge(y_ready, j + 1)
                pool.indirect_dma_start(yrows, bass.IndirectOffsetOnAxis(ap=sidx[:, j:j + 1], axis=0),
                                        yv[:, j % YRING], None).then_inc(scattered[j % YRING], 16)

            for b in (0, 2):
                pool.wait_ge(y2_ready, b + 1)
                y = y12[0][:, TT * b:TT * (b + 1)]
                g.tensor_tensor(y, y, mod[:, b, 5].unsqueeze(1).to_broadcast([P, TT, D]), ALU.mult
                                ).then_inc(yg_ready, 1)
                pool.wait_ge(yg_ready, b // 2 + 1)
                g.tensor_tensor(x1[:, b], y, x1[:, b], ALU.add).then_inc(yo_ready[b], 1)

        @block.scalar
        def _(act):
            a = nc.scalar
            with nc.allow_non_contiguous_dma(reason="small transposed and column loads"):
                act.dma_start(cT[:], c.rearrange("b d -> d b")).then_inc(s_c, 16)
                act.wait_ge(warm_ready, 1)
                a.activation(gt[:, 0, 0:1], warm[:, 0:1], ACT.Silu)
                act.dma_start(gqk[:, 0], g_q.partition_broadcast(P)).then_inc(s_gates, 16)
                act.dma_start(gqk[:, 1], g_k.partition_broadcast(P)).then_inc(s_gates, 16)
                act.wait_ge(s_c, 16)
                a.activation(siluc[:], cT[:], ACT.Silu).then_inc(silu_c_ready, 1)
                act.dma_start(gam[:], gamma.rearrange("(d a) -> d a", a=1)).then_inc(s_small, 16)
                act.dma_start(bet[:], beta.rearrange("(d a) -> d a", a=1)).then_inc(s_small, 16)
                act.dma_start(ws[:], Ws).then_inc(s_small, 16)
                act.dma_start(bsb[:], bs.partition_broadcast(P)).then_inc(s_small, 16)

            def gates(b):
                act.wait_ge(dots_ready, b + 1)
                if b >= 1:
                    act.wait_ge(gate_ready, b)
                a.activation(gt[:], dots[:], ACT.Tanh, scale=0.5).then_inc(gt_ready, 1)

            def full(*key):
                act.wait_ge(ring_full, USE[key] + 1)
                return R[:, USE[key] % 3]

            def turned_qk(b):
                for a, name in enumerate(("qT", "kT")):
                    r = full(name, b)
                    if b >= 1:
                        act.wait_ge(ring_full, USE[("k", b - 1, QUADS - 1)] + 1)
                    if b == 0:
                        act.wait_ge(spread_ready, 1)
                    a_hi = qkT_hi[:, a]
                    nc.scalar.activation(a_hi, r[:], ACT.Copy).then_inc(hi_ready, 1)

            def operand(b, i):
                r = full("q", b, i)
                if b >= 1:
                    act.wait_ge(scores_ready, 2 * (STEPS * (b - 1) + TT * (i + 1)))
                a.activation(QA[:, i], r[:], ACT.Copy).then_inc(ring_free_act, 1)

            def copy_mods(n0, n1):
                for n in range(n0, n1):
                    b, half = n // 2, n % 2
                    r = full("mod", b, half)
                    for m in range(3):
                        last = a.activation(mod[:, b, 3 * half + m], r[:, m * D:(m + 1) * D], ACT.Copy,
                                            bias=1.0 if m == 1 else 0.0)
                    last.then_inc(ring_free_act, 1)

            copy_mods(1, MODS_FIRST)
            act.wait_ge(wgate_ready, 1)
            for tt in range(TT):
                r = full("qkv", 0, tt)
                a.activation(sq[:, tt], r[:, 0:2 * D], ACT.Square).then_inc(sq_ready, 1)
                a.activation(proj[:, tt], r[:, 0:PROJ], ACT.Copy).then_inc(ring_free_act, 1)
            copy_mods(MODS_FIRST, 2 * B)
            gates(0)
            turned_qk(0)
            operand(0, 0)
            act.wait_ge(consts_ready, 1)
            for b in range(B):
                more = b + 1 < B
                for s in range(STEPS):
                    for pr in range(2):
                        n = 2 * (STEPS * b + s) + pr
                        act.wait_ge(scores_ready, n + 1)
                        if n >= 4:
                            act.wait_ge(av_done, (n - 4) // 2 + 1)
                        a.activation(tanh[:, n % 4], S[:, pr], ACT.Tanh, bias=tanh_bias[:, 0:1],
                                     scale=SHARPNESS).then_inc(tanh_ready, 1)
                    if b == 0 and s in FIRST_STEPS:
                        operand(0, 1 + FIRST_STEPS.index(s))
                    if s == GATE_STEP and more:
                        gates(b + 1)
                    if s == TURN_STEP and more:
                        turned_qk(b + 1)
                    if s in OPERAND_STEPS and more:
                        operand(b + 1, OPERAND_STEPS.index(s))
            act.wait_ge(dl_ready, 1)
            a.activation(th[:], dl[:], ACT.Tanh, scale=0.5).then_inc(th_ready, 1)

            act.wait_ge(tile_onehot_ready, 1)
            a.activation(hi1h[:, :, 0], hi1h[:, :, 2], ACT.Copy, scale=part1[:, 0:1]).then_inc(payload_ready, 1)

            def turn_hi(m):
                k0, k1 = turn_parts(m)
                act.wait_ge(turn_done, m + 4)
                a.activation(turned_hi[:, m % 3, k0:k1], turn_bank(m), ACT.Copy).then_inc(turned_hi_ready, 1)

            turn_hi(-3)
            turn_hi(-2)
            for j in range(SLOTS + 1):
                if j < SLOTS:
                    act.wait_ge(gu_ready, j + 1)
                    if j >= 2:
                        act.wait_ge(hid_ready, j - 1)
                    a.activation(sg[:, j % 2], S[:, j % 2, 0, 0:F], ACT.Silu).then_inc(silu_ready, 1)
                turn_hi(j - 1)
            for b in range(B):
                act.wait_ge(y_loaded[b], 16 * TOP)
                for tt in range(TT):
                    n = TT * b + tt
                    last = a.activation(y12[0][:, n], y12[0][:, n], ACT.Copy, scale=w12[:, 0, n:n + 1])
                last.then_inc(y1_ready, 1)

        @block.vector
        def _(dve):
            v = nc.vector
            chain = [0]

            def link(ins):
                chain[0] += 1
                ins.then_inc(dve_chain, 1)
                dve.wait_ge(dve_chain, chain[0])

            def full(*key):
                dve.wait_ge(ring_full, USE[key] + 1)
                return R[:, USE[key] % 3]

            dve.wait_ge(ident_ready, 1)
            v.memset(spread_f, 0.0)
            link(v.tensor_reduce(head32[:], ident[:].rearrange("p (i r) -> p r i", i=QUADS), AX_X, ALU.add))
            h4 = head32[:].rearrange("p (j d) -> p j d", d=HD).unsqueeze(2).to_broadcast([P, LANES, 2, HD])
            for k in range(2):
                v.tensor_copy(spread_f[:, k].rearrange("p (j u w d) -> p j u w d", j=LANES, u=2, w=2)[:, :, k], h4)
                last = v.tensor_copy(spread_f[:, 2 + k].rearrange(
                    "p (j u w d) -> p j u w d", j=LANES, u=2, w=2)[:, :, :, k], h4)
            link(last)
            v.tensor_copy(spread[:], spread_f).then_inc(spread_ready, 1)
            dve.wait_ge(silu_c_ready, 1)
            v.tensor_copy(silub, siluc[:].unsqueeze(2).to_broadcast([P, B, P])).then_inc(silu_b_ready, 1)
            def gate_columns():
                dve.wait_ge(s_wqkv, 48)
                dve.wait_ge(s_gates, 32)
                link(v.tensor_tensor(sq[:, 0].rearrange("p (a h d) -> p a h d", a=2, h=HEADS),
                                     wqk.rearrange("p (a h d) -> p a h d", a=2, h=HEADS),
                                     gqk[:].unsqueeze(2).to_broadcast([P, 2, HEADS, HD]), ALU.mult))
                v.tensor_reduce(wgate, sq[:, 0].rearrange("p (g d) -> p g d", d=HD), AX_X, ALU.add
                                ).then_inc(wgate_ready, 1)

            def mod_first():
                r = full("mod", 0, 0)
                v.tensor_copy(mod[:, 0, 0], r[:, 0:D])
                v.tensor_copy(mod[:, 0, 2], r[:, 2 * D:3 * D])
                v.tensor_scalar(mod[:, 0, 1], r[:, D:2 * D], 1.0, None, ALU.add).then_inc(ring_free, 1)
                dve.wait_ge(ring_free, 1)

            def mod_gates(half):
                m = mod[:, :, 3 * half + 2]
                dve.wait_ge(*freed("mod", B - 1, 1))
                if half == 1:
                    dve.wait_ge(mod_ready, 1)
                v.tensor_scalar(h2[:], m, 0.0, 0.5, ALU.is_ge, ALU.subtract)
                link(v.scalar_tensor_tensor(h2T[:], m, -1.0, m, ALU.mult, ALU.max))
                link(v.tensor_scalar(h2T[:], h2T[:], 0.25, 2.0, ALU.max, ALU.mult))
                v.tensor_tensor(m, h2[:], h2T[:], ALU.mult).then_inc(mod_ready, 1)

            def stats(src, st, mv, ve, var_sem):
                for tt in range(TT):
                    last = v.bn_stats(st[:, tt], src[:, tt])
                link(last)
                for tt in range(TT):
                    last = v.bn_aggr(mv[:, tt], st[:, tt])
                link(last)
                v.tensor_scalar(ve[:], mv[:, :, 1], LN_EPS, None, ALU.add).then_inc(var_sem, 1)

            def normalize(dst, src, mv, rstd, ready, n):
                dve.wait_ge(ready, n)
                for tt in range(TT):
                    last = v.tensor_scalar(dst[:, tt], src[:, tt], mv[:, tt, 0:1], rstd[:, tt:tt + 1],
                                           ALU.subtract, ALU.mult)
                return last

            def norms_center(b):
                dve.wait_ge(s_x[b], 16)
                stats(xin[:, b], st, mv, ve, var_ready)
                if b == 0:
                    mod_first()
                else:
                    dve.wait_ge(ring_full, USE[("hn", b - 1)] + 1)
                    dve.wait_ge(*freed("mod", b, 0))
                for tt in range(TT):
                    last = v.scalar_tensor_tensor(hh[:, tt], xin[:, b, tt], mv[:, tt, 0:1], mod[:, b, 1],
                                                  ALU.subtract, ALU.mult)
                link(last)

            def norms_h(b):
                dve.wait_ge(rstd_ready, 2 * b + 1)
                for tt in range(TT):
                    last = v.scalar_tensor_tensor(hh[:, tt], hh[:, tt], rstd[:, tt:tt + 1], mod[:, b, 0],
                                                  ALU.mult, ALU.add)
                last.then_inc(h_ready, 1)

            def norms_h_stats(b):
                dve.wait_ge(h_ready, b + 1)
                stats(hh, st, mv, ve, var_ready)

            def norms_hn(b):
                normalize(hn, hh, mv, rstd, rstd_ready, 2 * b + 2).then_inc(hn_ready, 1)

            def prep_hT(b):
                r = full("h", b)
                if b >= 1:
                    dve.wait_ge(ring_full, USE[("qkv", b - 1, TT - 1)] + 1)
                v.tensor_copy(hT.rearrange("p t d -> p (t d)"), r[:]).then_inc(ring_free, 1)

            def prep_xnT(b):
                if b == 0:
                    dve.wait_ge(s_small, 64)
                r = full("hn", b)
                v.tensor_scalar(xnT.rearrange("p t d -> p (t d)"), r[:], gam[:, 0:1], bet[:, 0:1], ALU.mult,
                                ALU.add).then_inc(ring_free, 1)

            def prep_qkv(b, tt):
                if b >= 1:
                    dve.wait_ge(gv_ready, b)
                    dve.wait_ge(ring_full, USE[("kT", b - 1)] + 1)
                r = full("qkv", b, tt)
                v.tensor_copy(proj[:, tt], r[:, 0:PROJ]).then_inc(ring_free, 1)

            def prep_rn(b):
                dve.wait_ge(sq_ready, TT + 2 * b)
                link(v.tensor_reduce(ss[:], sq[:].rearrange("p t (g d) -> p (t g) d", d=HD), AX_X, ALU.add))
                link(v.tensor_scalar(ss[:], ss[:], NORM_EPS * NORM_EPS, None, ALU.max))
                link(v.tensor_scalar(yt[:].bitcast(I32), ss[:].bitcast(I32), 1, None, ALU.arith_shift_right))
                if b >= 2:
                    dve.wait_ge(qn_ready, b - 1)
                v.tensor_scalar(yr[:].bitcast(I32), yt[:].bitcast(I32), -1.0, float(RSQRT_MAGIC),
                                ALU.mult, ALU.add)
                link(v.tensor_scalar(ss[:], ss[:], -0.5, None, ALU.mult))
                for it in range(3):
                    link(v.tensor_tensor(yt[:], yr[:], yr[:], ALU.mult))
                    link(v.tensor_tensor(yt[:], yt[:], ss[:], ALU.mult))
                    last = v.scalar_tensor_tensor(yr[:], yt[:], 1.5, yr[:], ALU.add, ALU.mult)
                    if it < 2:
                        link(last)
                last.then_inc(rn_ready, 1)
                dve.wait_ge(rn_ready, b + 1)

            def prep_dots(b):
                dve.wait_ge(*freed("qkv", b, TT - 1))
                if b >= 1:
                    dve.wait_ge(gt_ready, b)
                v.tensor_tensor(dots[:], proj[:, :, 2 * D:2 * D + NG], yr[:].rearrange("p (t g) -> p t g", t=TT),
                                ALU.mult).then_inc(dots_ready, 1)

            def prep_lo(b):
                for a, name in enumerate(("qT", "kT")):
                    dve.wait_ge(hi_ready, 2 * b + a + 1)
                    r = full(name, b)
                    v.tensor_tensor(qkT_lo[:, a], r[:], qkT_hi[:, a].bitcast(F32), ALU.subtract
                                    ).then_inc(ring_free, 1)

            def value_sums(b):
                dve.wait_ge(gv_ready, b + 1)
                if b >= 1:
                    dve.wait_ge(ring_full, USE[("csum", b - 1)] + 1)
                v.tensor_reduce(gvsum[:], gv[:].rearrange("p t q -> p q t"), AX_X, ALU.add).then_inc(gvsum_ready, 1)

            def value_operand(b, i):
                dve.wait_ge(gv_ready, b + 1)
                if b >= 1:
                    dve.wait_ge(av_done, STEPS * (b - 1) + TT * (i + 1))
                v.tensor_copy(gvz[:, :, i, :, HD * i:HD * (i + 1)],
                              gv[:].rearrange("p t (j i d) -> p t j i d", j=LANES, d=HD)[:, :, :, i]
                              ).then_inc(gvz_ready, 1)

            def prep_gates(b):
                dve.wait_ge(gt_ready, b + 1)
                if b >= 1:
                    dve.wait_ge(gqe_ready, b)
                v.tensor_scalar(gate[:, :, 0:HEADS], gt[:, :, 0:HEADS], 0.375, 0.625, ALU.mult, ALU.add)
                v.tensor_scalar(gate[:, :, HEADS:NG], gt[:, :, HEADS:NG], 0.1875, 0.3125, ALU.mult, ALU.add
                                ).then_inc(gate_ready, 1)

            def prep_gqt(b):
                r = full("gate", b)
                v.tensor_copy(GQT[:], r[:]).then_inc(ring_free, 1)
                r = full("csum", b)
                v.tensor_copy(Cs[:], r[:, 0:1]).then_inc(ring_free, 1)

            def prep_operands(b, i):
                if b >= 1:
                    dve.wait_ge(scores_ready, 2 * (STEPS * (b - 1) + TT * (i + 1)))
                r = full("k", b, i)
                v.tensor_copy(KA[:, i], r[:]).then_inc(ring_free, 1)

            def fuse(b):
                dve.wait_ge(av_done, STEPS * (b + 1))
                if b >= 1:
                    dve.wait_ge(ring_full, USE[("wo", b - 1)] + 1)
                dve.wait_ge(*freed("csum", b))
                v.scalar_tensor_tensor(fT[:], AV[:], Cs[:, 0:1], GQT[:], ALU.add, ALU.mult).then_inc(fused_ready, 1)

            def post_x1(b):
                r = full("wo", b)
                dve.wait_ge(xb_ready, b + 1)
                v.tensor_tensor(x1[:, b], r[:].rearrange("p (t d) -> p t d", t=TT), xb[:], ALU.add
                                ).then_inc(ring_free, 1)
                dve.wait_ge(*freed("wo", b))
                stats(x1[:, b], st2, mv2, ve2, var2_ready)

            def post_center(b):
                if b >= 1:
                    dve.wait_ge(ring_full, USE[("h2T", b - 1)] + 1)
                    dve.wait_ge(h2_stored, 16 * b)
                for tt in range(TT):
                    last = v.scalar_tensor_tensor(h2[:, tt], x1[:, b, tt], mv2[:, tt, 0:1], mod[:, b, 4],
                                                  ALU.subtract, ALU.mult)
                link(last)

            def post_norm(b):
                dve.wait_ge(rstd2_ready, b + 1)
                for tt in range(TT):
                    last = v.scalar_tensor_tensor(h2[:, tt], h2[:, tt], rstd2[:, tt:tt + 1], mod[:, b, 3],
                                                  ALU.mult, ALU.add)
                last.then_inc(h2_ready, 1)

            def post_h2(b):
                r = full("h2T", b)
                if b >= 1:
                    dve.wait_ge(ring_full, USE[("logit", b - 1)] + 1)
                v.tensor_copy(h2T[:].rearrange("p t d -> p (t d)"), r[:]).then_inc(ring_free, 1)

            def post_logit(b):
                r = full("logit", b)
                v.tensor_tensor(lg[:, TT * b:TT * (b + 1)], r[:, 0:TT * E].rearrange("p (t e) -> p t e", e=E),
                                bsb[:].unsqueeze(1).to_broadcast([P, TT, E]), ALU.add).then_inc(ring_free, 1)
                dve.wait_ge(*freed("logit", b))

            def choose(b):
                n0, n1 = TT * b, TT * (b + 1)
                for n in range(n0, n1):
                    last = v.max(top[:, n], lg[:, n])
                link(last)
                for n in range(n0, n1):
                    last = v.max_index(topi[:, n], top[:, n], lg[:, n])
                link(last)
                link(v.tensor_copy(topf[:, n0:n1], topi[:, n0:n1]))
                for k in range(TOP):
                    last = v.tensor_tensor(oh[:, k, n0:n1], iota8[:].unsqueeze(1).to_broadcast([P, TT, E]),
                                           topf[:, n0:n1, k:k + 1].to_broadcast([P, TT, E]), ALU.is_equal)
                link(last)
                link(v.tensor_tensor(pick[:, n0:n1], oh[:, 0, n0:n1], oh[:, 1, n0:n1], ALU.add))
                for n in range(n0, n1):
                    last = v.tensor_tensor(before[:, n + 1], before[:, n], pick[:, n], ALU.add)
                    if n == NT - 1:
                        last.then_inc(counts_ready, 1)
                    else:
                        link(last)

            def weights(n):
                dve.wait_ge(s_raw[n % 2], raw_count(n))
                if n < NW:
                    hi = (wgh, wuh)[n // E]
                    v.tensor_copy(hi[:, n % E], wraw[:, n % 2, 0:F]).then_inc(wsplit, 1)
                else:
                    v.tensor_copy(wd[:, n - NW, :, 0], wraw[:, n % 2].rearrange("p (k d) -> p k d", d=D)
                                  ).then_inc(wsplit, 1)

            def raw_count(n):
                return 16 * sum(1 if m < NW else 2 for m in range(n % 2, n + 1, 2))

            norms_center(0)
            norms_h(0)
            norms_h_stats(0)
            gate_columns()
            prep_hT(0)
            norms_hn(0)
            prep_xnT(0)
            norms_center(1)
            prep_rn(0)
            q = proj[:, :, 0:2 * D].rearrange("p t (g d) -> p t g d", d=HD)
            prep_dots(0)
            v.tensor_tensor(q, q, yr[:].rearrange("p (t g) -> p t g", t=TT).unsqueeze(3).to_broadcast(
                [P, TT, NG, HD]), ALU.mult).then_inc(qn_ready, 1)
            prep_gates(0)
            norms_h(1)
            prep_lo(0)
            norms_h_stats(1)
            prep_operands(0, 0)
            norms_hn(1)
            for i in range(QUADS):
                value_operand(0, i)
            value_sums(0)
            dve.wait_ge(consts_ready, 1)
            for b in range(B):
                more = b + 1 < B
                n = 3 * E // B * b
                if b >= 1:
                    fuse(b - 1)
                if more:
                    prep_hT(b + 1)
                    prep_xnT(b + 1)
                if b >= 1:
                    value_operand(b, QUADS - 1)
                if more:
                    prep_qkv(b + 1, 0)
                weights(n)
                if b >= 1:
                    post_x1(b - 1)
                else:
                    prep_operands(0, 1)
                if more:
                    prep_qkv(b + 1, 1)
                if b >= 1:
                    post_center(b - 1)
                if more:
                    prep_qkv(b + 1, 2)
                if b >= 1:
                    post_norm(b - 1)
                if more:
                    prep_qkv(b + 1, 3)
                weights(n + 1)
                if b == 0:
                    prep_operands(0, 2)
                prep_gqt(b)
                if b == 0:
                    prep_operands(0, 3)
                if more:
                    prep_rn(b + 1)
                    prep_dots(b + 1)
                if b >= 1:
                    post_h2(b - 1)
                if b + 2 < B:
                    norms_center(b + 2)
                weights(n + 2)
                if more:
                    prep_gates(b + 1)
                if b >= 1:
                    post_logit(b - 1)
                if more:
                    prep_lo(b + 1)
                if b + 2 < B:
                    norms_h(b + 2)
                    norms_h_stats(b + 2)
                weights(n + 3)
                if b >= 1:
                    choose(b - 1)
                if b == 0:
                    mod_gates(0)
                    mod_gates(1)
                    dve.wait_ge(mod_ready, 2)
                    dve.wait_ge(s_wo, 16 * HEADS)
                    v.tensor_tensor(wog[:], wo[:].unsqueeze(1).to_broadcast([P, B, D]), mod[:, :, 2],
                                    ALU.mult).then_inc(wog_ready, 1)
                if b + 2 < B:
                    norms_hn(b + 2)
                weights(n + 4)
                if more:
                    prep_operands(b + 1, 0)
                    for i in range(QUADS - 1):
                        value_operand(b + 1, i)
                    value_sums(b + 1)
                weights(n + 5)
                if more:
                    for i in range(1, QUADS):
                        prep_operands(b + 1, i)
            fuse(B - 1)
            post_x1(B - 1)
            post_center(B - 1)
            post_norm(B - 1)
            post_h2(B - 1)
            post_logit(B - 1)
            choose(B - 1)
            dve.wait_ge(*freed("logit", B - 1))
            v.tensor_tensor(dl[:], top[:, :, 0], top[:, :, 1], ALU.subtract).then_inc(dl_ready, 1)
            dve.wait_ge(rank_ready, 1)
            rank, total = R[:, 0, 0:NT * E], R[:, 0, NT * E:NT * E + E]
            link(v.tensor_scalar(toti[:], total, float(P - 1), None, ALU.add))
            link(v.tensor_scalar(toti[:], toti[:], 7, None, ALU.arith_shift_right))
            link(v.tensor_copy(tot[:, 0], toti[:]))
            cur = 0
            for step in (1, 2, 4):
                v.tensor_copy(tot[:, cur + 1, 0:step], tot[:, cur, 0:step])
                link(v.tensor_tensor(tot[:, cur + 1, step:E], tot[:, cur, step:E], tot[:, cur, 0:E - step], ALU.add))
                cur += 1
            link(v.tensor_tensor(tbase[:], tot[:, 3], tot[:, 0], ALU.subtract))
            link(v.tensor_scalar(tbase[:], tbase[:], float(P), None, ALU.mult))
            link(v.tensor_tensor(slot3[:], rank.rearrange("p (n e) -> p n e", e=E),
                                 tbase[:].unsqueeze(1).to_broadcast([P, NT, E]), ALU.add))
            for k in range(TOP):
                last = v.tensor_tensor(slotm[:, k], oh[:, k], slot3[:], ALU.mult)
            link(last)
            link(v.tensor_reduce(slot[:], slotm[:].rearrange("p k n e -> p (k n) e"), AX_X, ALU.add))
            link(v.tensor_copy(sloti[:, 0], slot[:]))
            v.tensor_scalar(sloti[:, 1], sloti[:, 0], P - 1, None, ALU.bitwise_and)
            link(v.tensor_scalar(sloti[:, 2], sloti[:, 0], 7, None, ALU.arith_shift_right))
            v.tensor_copy(slot_tile[:], sloti[:, 2])
            v.tensor_copy(slot_row[:], sloti[:, 1]).then_inc(slot_ready, 1)
            dve.wait_ge(slot_ready, 1)
            v.tensor_tensor(hi1h[:, :, 2], iotas[:].unsqueeze(1).to_broadcast([P, NK, SLOTS]),
                            slot_tile[:].unsqueeze(2).to_broadcast([P, NK, SLOTS]), ALU.is_equal
                            ).then_inc(tile_onehot_ready, 1)
            dve.wait_ge(tile_onehot_ready, 1)
            v.tensor_tensor(hi1h[:, :, 1], hi1h[:, :, 2], picks[:].unsqueeze(2).to_broadcast([P, NK, SLOTS]),
                            ALU.mult).then_inc(payload_ready, 1)
            for n in range(ROWS_POOL, NK):
                v.tensor_scalar(lo1h[:, n], iotap[:], slot_row[:, n:n + 1], None,
                                ALU.is_equal).then_inc(onehot_ready, 1)
            link(v.tensor_tensor(eotc[:], iotas[:].unsqueeze(2).to_broadcast([P, SLOTS, E]),
                                 tot[:, 3].unsqueeze(1).to_broadcast([P, SLOTS, E]), ALU.is_ge))
            link(v.tensor_reduce(eotf[:], eotc[:], AX_X, ALU.add))
            v.tensor_scalar(eot[:], eotf[:], float(E - 1), None, ALU.min).then_inc(idx_ready, 1)
            dve.wait_ge(inv_ready, 1)
            got = R[:, 1, 0:2 * SLOTS].rearrange("p (a j) -> p a j", a=2)
            link(v.tensor_copy(inv[:, 0], got[:, 0]))
            link(v.scalar_tensor_tensor(inv[:, 1], got[:, 1], float(P), inv[:, 0], ALU.mult, ALU.add))
            link(v.tensor_scalar(gnum[:], inv[:, 1], 1.0, 0.0, ALU.subtract, ALU.max))
            v.tensor_scalar(gidx[:], gnum[:], NT * P - 1, None, ALU.bitwise_and).then_inc(idx_ready, 1)
            link(v.scalar_tensor_tensor(inv[:, 2], inv[:, 1], 0.0, spare[:], ALU.is_equal, ALU.mult))
            v.scalar_tensor_tensor(sidx[:], inv[:, 1], -1.0, inv[:, 2], ALU.add, ALU.add).then_inc(idx_ready, 1)
            dve.wait_ge(th_ready, 1)
            v.tensor_scalar(w12[:, 0], th[:], 0.5, 0.5, ALU.mult, ALU.add)
            link(v.tensor_scalar(w12[:, 1], th[:], -0.5, 0.5, ALU.mult, ALU.add))

            v.memset(hid[:, :, F:FC * P], 0.0)

            def turn_lo(m):
                k0, k1 = turn_parts(m)
                dve.wait_ge(turned_hi_ready, m + 4)
                v.tensor_tensor(turned_lo[:, m % 3, k0:k1], turn_bank(m),
                                turned_hi[:, m % 3, k0:k1].bitcast(F32), ALU.subtract).then_inc(turned_lo_ready, 1)

            turn_lo(-3)
            turn_lo(-2)
            for j in range(SLOTS + 2):
                if j < SLOTS:
                    dve.wait_ge(silu_ready, j + 1)
                    if j >= 2:
                        dve.wait_ge(turn_done, j + 2)
                    v.tensor_tensor(hid[:, j % 2, 0:F], sg[:, j % 2], S[:, j % 2, 1, 0:F],
                                    ALU.mult).then_inc(hid_ready, 1)
                if j <= SLOTS:
                    turn_lo(j - 1)
                if j >= 2:
                    m = j - 2
                    dve.wait_ge(down_done, m + 1)
                    if m >= YRING:
                        dve.wait_ge(scattered[m % YRING], 16 * (m // YRING))
                    v.tensor_reduce(yv[:, m % YRING], R[:, m % 2, 0:2 * D].rearrange("p (u d) -> p d u", u=2),
                                    AX_X, ALU.add).then_inc(y_ready, 1)

            def add_second(b):
                dve.wait_ge(y1_ready, b + 1)
                for tt in range(TT):
                    n = TT * b + tt
                    last = v.scalar_tensor_tensor(y12[0][:, n], y12[1][:, n], w12[:, 1, n:n + 1], y12[0][:, n],
                                                  ALU.mult, ALU.add)
                last.then_inc(y2_ready, 1)
                dve.wait_ge(y2_ready, b + 1)

            def finish(b):
                y = y12[0][:, TT * b:TT * (b + 1)]
                link(v.tensor_tensor(y, y, mod[:, b, 5].unsqueeze(1).to_broadcast([P, TT, D]), ALU.mult))
                v.tensor_tensor(x1[:, b], y, x1[:, b], ALU.add).then_inc(yo_ready[b], 1)

            add_second(0)
            add_second(1)
            finish(1)
            add_second(2)
            add_second(3)
            finish(3)

        @block.tensor
        def _(pe):
            mm = nc.tensor.matmul

            def claim(*key):
                n = USE[key]
                if n >= 3:
                    pe.wait_ge(*freed(*order[n - 3]))
                return R[:, n % 3]

            pe.wait_ge(silu_b_ready, 1)
            pe.wait_ge(s_wm, 16)
            def transposes(key, src):
                r = claim(*key)
                for tt in range(TT):
                    last = nc.tensor.transpose(r[:, tt * P:(tt + 1) * P], src(tt), ident[:])
                last.then_inc(ring_full, 1)

            def prep_x(b):
                pe.wait_ge(h_ready, b + 1)
                transposes(("h", b), lambda tt: hh[:, tt])
                if b == 0:
                    heat(AV[:], HEAT_START[0])
                pe.wait_ge(hn_ready, b + 1)
                transposes(("hn", b), lambda tt: hn[:, tt])

            def prep_qkv(b, tt):
                r = claim("qkv", b, tt)
                pe.wait_ge(*freed("hn", b))
                mm(r[:, 0:2 * D + NG], xnT[:, tt], wproj[:, 0:2 * D + NG], start=True, stop=True)
                mm(r[:, 2 * D + NG:PROJ], hT[:, tt], wvp, start=True, stop=True).then_inc(ring_full, 1)

            def prep_gate(b):
                pe.wait_ge(gqe_ready, b + 1)
                transposes(("gate", b), lambda tt: gqe[:, tt])
                r = claim("csum", b)
                heat(r[:], HEAT_SUMS)
                pe.wait_ge(gvsum_ready, b + 1)
                mm(r[:, 0:1], gvsum[:], ones[:], start=True, stop=True).then_inc(ring_full, 1)

            def turn_qk(b):
                pe.wait_ge(qn_ready, b + 1)
                transposes(("qT", b), lambda tt: proj[:, tt, 0:D])
                transposes(("kT", b), lambda tt: proj[:, tt, D:2 * D])

            def prep_operand(b, i):
                rows = slice(32 * i, 32 * i + 32)
                pe.wait_ge(*freed("kT", b))
                for name, a in (("q", 0), ("k", 1)):
                    r = claim(name, b, i)
                    mm(r[:], spread[rows, 2 * a], qkT_hi[rows, a], start=True, stop=False)
                    mm(r[:], spread[rows, 2 * a + 1], qkT_lo[rows, a], start=False, stop=True
                       ).then_inc(ring_full, 1)

            def scores(b, s):
                i, kt = s // TT, s % TT
                if kt == 0:
                    pe.wait_ge(*freed("q", b, i))
                    pe.wait_ge(*freed("k", b, i))
                for pr in range(2):
                    n = 2 * (STEPS * b + s) + pr
                    if n >= 2:
                        pe.wait_ge(tanh_ready, n - 1)
                    if pr == 0 and (s in HEAT_STEPS or b == s == 0):
                        heat(S[:, 0, 0], 1)
                    for u in range(2):
                        r0 = 32 * (2 * pr + u)
                        last = mm(S[:, pr, u], KA[r0:r0 + 32, i, kt * P:(kt + 1) * P], QA[r0:r0 + 32, i, :],
                                  start=True, stop=True)
                    last.then_inc(scores_ready, 1)

            def values(b, s):
                i, kt = s // TT, s % TT
                if s == 0 and b >= 1:
                    pe.wait_ge(fused_ready, b)
                if kt == 0:
                    pe.wait_ge(gvz_ready, QUADS * b + i + 1)
                for lane in range(LANES):
                    n = 2 * (STEPS * b + s) + lane // 2
                    pe.wait_ge(tanh_ready, n + 1)
                    last = mm(AV[32 * lane:32 * lane + 32, :], gvz[:, kt, i, lane], tanh[:, n % 4, lane % 2],
                              start=s == 0, stop=s == STEPS - 1)
                last.then_inc(av_done, 1)

            def post(b, part):
                if part == 0:
                    pe.wait_ge(fused_ready, b + 1)
                    r = claim("wo", b)
                    for tt in range(TT):
                        last = mm(r[:, tt * P:(tt + 1) * P], fT[:, tt * P:(tt + 1) * P], wog[:, b], start=True, stop=True)
                    last.then_inc(ring_full, 1)
                elif part == 1:
                    pe.wait_ge(h2_ready, b + 1)
                    transposes(("h2T", b), lambda tt: h2[:, tt])
                else:
                    r = claim("logit", b)
                    pe.wait_ge(*freed("h2T", b))
                    for tt in range(TT):
                        last = mm(r[:, tt * E:(tt + 1) * E], h2T[:, tt], ws[:], start=True, stop=True)
                    last.then_inc(ring_full, 1)

            def heat(to, count):
                for _ in range(count):
                    mm(to, warm[:, 0:P], warm[:], start=True, stop=True)

            def mods(n0, n1):
                for n in range(n0, n1):
                    b, half = n // 2, n % 2
                    r = claim("mod", b, half)
                    mm(r[:, 0:3 * D], silub[:, b], wm[:, 3 * half * D:3 * (half + 1) * D], start=True,
                       stop=True).then_inc(ring_full, 1)

            mods(0, MODS_FIRST)
            pe.wait_ge(ident_ready, 1)
            pe.wait_ge(warm_ready, 1)
            prep_x(0)
            pe.wait_ge(wvp_ready, 1)
            pe.wait_ge(wgate_ready, 1)
            for tt in range(TT):
                prep_qkv(0, tt)
            mods(MODS_FIRST, 2 * B)
            pe.wait_ge(consts_ready, 1)
            heat(AV[:], HEAT_START[1])
            turn_qk(0)
            heat(AV[:], HEAT_START[2])
            prep_operand(0, 0)
            for b in range(B):
                more = b + 1 < B
                for s in range(STEPS):
                    scores(b, s)
                    if b == s == 0:
                        heat(AV[:], HEAT_START[3])
                    if s > 0:
                        values(b, s - 1)
                    elif b > 0:
                        values(b - 1, STEPS - 1)
                    if s == 0 and more:
                        prep_x(b + 1)
                    if s == 2 and b >= 1:
                        pe.wait_ge(wog_ready, 1)
                        post(b - 1, 0)
                    if s in (1, 2, 3, 4) and more:
                        prep_qkv(b + 1, s - 1)
                    if b == 0 and s in FIRST_STEPS[:2]:
                        prep_operand(0, 1 + FIRST_STEPS.index(s))
                    if s == 5:
                        prep_gate(b)
                    if b == 0 and s == FIRST_STEPS[2]:
                        prep_operand(0, 3)
                    if s in POST_STEPS and b >= 1:
                        post(b - 1, 1 + POST_STEPS.index(s))
                    if more and s == TURN_STEP:
                        turn_qk(b + 1)
                    if more and s in OPERAND_STEPS:
                        prep_operand(b + 1, OPERAND_STEPS.index(s))
            values(B - 1, STEPS - 1)
            for part in range(3):
                post(B - 1, part)
                heat(AV[:], HEAT_COUNTS[part])

            pe.wait_ge(counts_ready, 1)
            rank = R[:, 0, 0:NT * E]
            mm(rank, onesq[:], before[:, 0:NT].rearrange("p n e -> p (n e)"), start=True, stop=False)
            mm(rank, tri[:], pick[:].rearrange("p n e -> p (n e)"), start=False, stop=True)
            mm(R[:, 0, NT * E:NT * E + E], onesq[:], before[:, NT], start=True, stop=True).then_inc(rank_ready, 1)
            heat(AV[:], HEAT_COUNTS[3])
            pe.wait_ge(payload_ready, 2)
            for n in range(NK):
                if n < ROWS_POOL:
                    pe.wait_ge(onehot_pool_ready, n + 1)
                else:
                    pe.wait_ge(onehot_ready, n - ROWS_POOL + 1)
                last = mm(R[:, 1, 0:2 * SLOTS], lo1h[:, n], hi1h[:, n, 0:2].rearrange("p a j -> p (a j)"),
                          start=n == 0, stop=n == NK - 1)
            last.then_inc(inv_ready, 1)

            heat(AV[:], HEAT_COUNTS[4])

            pe.wait_ge(wlo, 3 * E)
            pe.wait_ge(idx_ready, 2)

            def expert(j):
                return nc.tensor.value_load(eot[0:1, j:j + 1], min_val=0, max_val=E - 1)

            def up(j, e):
                pe.wait_ge(turned_lo_ready, j + 1)
                if j >= 2:
                    pe.wait_ge(hid_ready, j - 1)
                G, U = S[:, j % 2, 0, 0:F], S[:, j % 2, 1, 0:F]
                hi, lo = turned_hi[:, j % 3, FC], turned_lo[:, j % 3, FC]

                def w(t):
                    return t[:, bass.ds(e, 1)].rearrange("p a f -> p (a f)")

                mm(G, hi, w(wgh), start=True, stop=False)
                mm(G, hi, w(wgl), start=False, stop=False)
                mm(U, hi, w(wuh), start=True, stop=False)
                mm(U, hi, w(wul), start=False, stop=False)
                mm(G, lo, w(wgh), start=False, stop=True)
                mm(U, lo, w(wuh), start=False, stop=True).then_inc(gu_ready, 1)

            def turn(m):
                if m >= -1:
                    pe.wait_ge(turned_lo_ready, m + 2)
                if m >= 0:
                    pe.wait_ge(hid_ready, m + 1)
                if m + 3 < SLOTS:
                    pe.wait_ge(gathered[(m + 3) % XRING], 16 * ((m + 3) // XRING + 1))
                k0, k1 = turn_parts(m)
                for k in range(k0, k1):
                    src = hid[:, m % 2, k * P:(k + 1) * P] if k < FC else xg[:, (m + 3) % XRING]
                    last = nc.tensor.transpose(turn_bank(m)[:, k - k0], src, ident[:])
                last.then_inc(turn_done, 1)

            def down(j, e):
                pe.wait_ge(turned_lo_ready, j + 4)
                if j >= 2:
                    pe.wait_ge(y_ready, j - 1)
                y = R[:, j % 2, 0:2 * D]
                for k in range(FC):
                    rows = P if k < FC - 1 else FLAST
                    hi, lo = turned_hi[0:rows, j % 3, k], turned_lo[0:rows, j % 3, k]
                    w = wd[0:rows, bass.ds(e, 1), k].rearrange("p a u d -> p a (u d)")
                    both = (y, hi, w.rearrange("p a d -> p (a d)"))
                    one = (y[:, 0:D], lo, w[:, :, 0:D].rearrange("p a d -> p (a d)"))
                    if k < FC - 1:
                        mm(*both, start=k == 0, stop=False)
                        mm(*one, start=False, stop=False)
                    else:
                        mm(*one, start=False, stop=False)
                        mm(*both, start=False, stop=True).then_inc(down_done, 1)

            es = {}
            turn(-3)
            turn(-2)
            for j in range(SLOTS + 2):
                if j < SLOTS:
                    es[j] = expert(j)
                    up(j, es[j])
                if j <= SLOTS:
                    turn(j - 1)
                if j >= 2:
                    down(j - 2, es[j - 2])


_INS = ["x", "w_q", "w_k", "w_v", "g_q", "g_k", "w_o", "b_o", "gamma", "beta"]
_FFN = ["Ws", "bs", "Wg", "Wu", "Wd"]


def kernel(**inputs):
    import numpy as np
    import concourse.bacc as bacc
    from concourse.bass_utils import run_bass_kernel_spmd

    nc = bacc.Bacc("TRN2", target_bir_lowering=False, num_devices=1)
    names = ["L0_attn_" + n for n in _INS] + ["L0_ffn_" + n for n in _FFN] + ["L0_c", "L0_wmod"]
    arrays, args = {}, []
    for name in names:
        a = np.ascontiguousarray(inputs[name])
        arrays[f"in_{name}"] = a
        args.append(nc.dram_tensor(f"in_{name}", a.shape, mybir.dt.from_np(a.dtype), kind="ExternalInput").ap())
    out = nc.dram_tensor("out_x", arrays["in_L0_attn_x"].shape, F32, kind="ExternalOutput").ap()
    adaln_block(nc, *args, out)
    r = run_bass_kernel_spmd(nc, [arrays], core_ids=[0])
    return r.results[0]["out_x"]
```
